# Optimizing a Trainium2 kernel written in Bass

```python
import numpy as np
import jax
import jax.numpy as jnp

def _softmax(x, axis=-1):
    return jax.nn.softmax(x, axis=axis)

def _gelu(x):
    return jax.nn.gelu(x, approximate=True)

def _silu(x):
    return jax.nn.silu(x)

def _sigmoid(x):
    return jax.nn.sigmoid(x)

def _layernorm(x, axis=-1, eps=1e-05):
    m = jnp.mean(x, axis=axis, keepdims=True)
    v = jnp.var(x, axis=axis, keepdims=True)
    return (x - m) / jnp.sqrt(v + eps)

def _scatter_add(tgt, idx, src, axis=0):
    return tgt.at[idx].add(src)

def _segment_sum(src, seg, n):
    return jax.ops.segment_sum(src, seg, n)
kernel_name = 'mk_sandwich_d1_jaxref_r8_29403e'

def setup_inputs(seed: int=0):
    np.random.seed(seed)
    _w = jnp.asarray

    def _L0_attn_setup():
        import jax, jax.numpy as jnp
        import numpy as np
        import math
        B, L, D, H = (32, 64, 512, 32)
        HD = D // H
        key = jax.random.key(seed)
        ks = jax.random.split(key, 9)
        s = 1.0 / math.sqrt(D)
        return {'x': jax.random.normal(ks[0], (B, L, D), jnp.float32), 'Wq': jax.random.normal(ks[1], (D, D), jnp.float32) * s, 'bq': jax.random.normal(ks[2], (D,), jnp.float32) * s, 'Wk': jax.random.normal(ks[3], (D, D), jnp.float32) * s, 'bk': jax.random.normal(ks[4], (D,), jnp.float32) * s, 'Wv': jax.random.normal(ks[5], (D, D), jnp.float32) * s, 'bv': jax.random.normal(ks[6], (D,), jnp.float32) * s, 'Wo': jax.random.normal(ks[7], (D, D), jnp.float32) * s, 'bo': jax.random.normal(ks[8], (D,), jnp.float32) * s}
    _L0_attn_in = _L0_attn_setup()

    def _L0_ffn_setup():
        import jax, jax.numpy as jnp
        import numpy as np
        THRESH_FACTOR = 0.7

        def _bitlinear(x, w, scale):
            w_abs = jnp.abs(w)
            thr = jnp.mean(w_abs) * THRESH_FACTOR
            wq = jnp.sign(w) * (w_abs > thr).astype(w.dtype)
            w_scaled = wq * scale
            return jnp.einsum('bsd,od->bso', x, w_scaled)
        key = jax.random.key(seed)
        k1, k2, k3, k4 = jax.random.split(key, 4)
        dim, hidden = (512, 2048)
        x = jax.random.normal(k1, (2, 256, dim), dtype=jnp.float32)
        gate_w = jax.random.normal(k2, (hidden, dim), dtype=jnp.float32) / np.sqrt(dim)
        up_w = jax.random.normal(k3, (hidden, dim), dtype=jnp.float32) / np.sqrt(dim)
        down_w = jax.random.normal(k4, (dim, hidden), dtype=jnp.float32) / np.sqrt(hidden)
        return {'x': x, 'gate_w': gate_w, 'gate_scale': jnp.ones((hidden, 1), jnp.float32), 'up_w': up_w, 'up_scale': jnp.ones((hidden, 1), jnp.float32), 'down_w': down_w, 'down_scale': jnp.ones((dim, 1), jnp.float32)}
    _L0_ffn_in = _L0_ffn_setup()
    _d = {'L0_attn_x': _L0_attn_in['x'], 'L0_attn_Wq': _L0_attn_in['Wq'], 'L0_attn_bq': _L0_attn_in['bq'], 'L0_attn_Wk': _L0_attn_in['Wk'], 'L0_attn_bk': _L0_attn_in['bk'], 'L0_attn_Wv': _L0_attn_in['Wv'], 'L0_attn_bv': _L0_attn_in['bv'], 'L0_attn_Wo': _L0_attn_in['Wo'], 'L0_attn_bo': _L0_attn_in['bo'], 'L0_ffn_gate_w': _L0_ffn_in['gate_w'], 'L0_ffn_gate_scale': _L0_ffn_in['gate_scale'], 'L0_ffn_up_w': _L0_ffn_in['up_w'], 'L0_ffn_up_scale': _L0_ffn_in['up_scale'], 'L0_ffn_down_w': _L0_ffn_in['down_w'], 'L0_ffn_down_scale': _L0_ffn_in['down_scale']}
    _x0 = _d['L0_attn_x']
    _d['L0_attn_x'] = jax.random.normal(jax.random.fold_in(jax.random.key(seed), 1), (2, 512, 512), dtype=_x0.dtype)
    del _x0
    return _d

def reference(L0_attn_x, L0_attn_Wq, L0_attn_bq, L0_attn_Wk, L0_attn_bk, L0_attn_Wv, L0_attn_bv, L0_attn_Wo, L0_attn_bo, L0_ffn_gate_w, L0_ffn_gate_scale, L0_ffn_up_w, L0_ffn_up_scale, L0_ffn_down_w, L0_ffn_down_scale):

    def _L0_attn_ref(x, Wq, bq, Wk, bk, Wv, bv, Wo, bo):
        import jax, jax.numpy as jnp
        import numpy as np
        import math
        B, L, D, H = (32, 64, 512, 32)
        HD = D // H
        b, l, d = x.shape
        h, hd = (H, HD)
        q = (x @ Wq.T + bq).reshape(b, l, h, hd).transpose(0, 2, 1, 3)
        k = (x @ Wk.T + bk).reshape(b, l, h, hd).transpose(0, 2, 1, 3)
        v = (x @ Wv.T + bv).reshape(b, l, h, hd).transpose(0, 2, 1, 3)
        scores = jnp.einsum('bhqd,bhkd->bhqk', q, k) / math.sqrt(hd)
        causal = jnp.tril(jnp.ones((l, l), bool))
        scores = jnp.where(causal, scores, -jnp.inf)
        att = jax.nn.softmax(scores, axis=-1)
        out = jnp.einsum('bhqk,bhkd->bhqd', att, v)
        out = out.transpose(0, 2, 1, 3).reshape(b, l, d)
        return out @ Wo.T + bo

    def _L0_ffn_ref(x, gate_w, gate_scale, up_w, up_scale, down_w, down_scale):
        import jax, jax.numpy as jnp
        import numpy as np
        THRESH_FACTOR = 0.7

        def _bitlinear(x, w, scale):
            w_abs = jnp.abs(w)
            thr = jnp.mean(w_abs) * THRESH_FACTOR
            wq = jnp.sign(w) * (w_abs > thr).astype(w.dtype)
            w_scaled = wq * scale
            return jnp.einsum('bsd,od->bso', x, w_scaled)
        gate = _bitlinear(x, gate_w, gate_scale)
        up = _bitlinear(x, up_w, up_scale)
        hidden = jax.nn.silu(gate) * up
        out = _bitlinear(hidden, down_w, down_scale)
        return out
    x = L0_attn_x
    x = x + _layernorm(_L0_attn_ref(_layernorm(x, axis=-1), L0_attn_Wq, L0_attn_bq, L0_attn_Wk, L0_attn_bk, L0_attn_Wv, L0_attn_bv, L0_attn_Wo, L0_attn_bo), axis=-1)
    x = x + _layernorm(_L0_ffn_ref(_layernorm(x, axis=-1), L0_ffn_gate_w, L0_ffn_gate_scale, L0_ffn_up_w, L0_ffn_up_scale, L0_ffn_down_w, L0_ffn_down_scale), axis=-1)
    return x

_drawn_inputs = setup_inputs


def setup_inputs(seed=0):
    import zlib

    import numpy as np

    out = dict(_drawn_inputs(seed))
    spreads = {'L0_ffn_gate_scale': (1.0, 0.2),
     'L0_ffn_up_scale': (1.0, 0.2),
     'L0_ffn_down_scale': (1.0, 0.2)}
    factors = {}
    for name, (base, spread) in spreads.items():
        noise = np.random.default_rng([zlib.crc32(name.encode()), seed]).standard_normal(out[name].shape)
        drawn = base * np.exp(spread * noise) if base else spread * noise
        out[name] = jnp.asarray(drawn.astype(out[name].dtype))
    for name, factor in factors.items():
        out[name] = (out[name] * factor).astype(out[name].dtype)
    return out
```

```python
from contextlib import ExitStack

import concourse.bass as bass
from concourse import mybir

F32 = mybir.dt.float32
F32R = mybir.dt.float32r
BF16 = mybir.dt.bfloat16
F16 = mybir.dt.float16
I32 = mybir.dt.int32
ALU = mybir.AluOpType
ACT = mybir.ActivationFunctionType
AX = mybir.AxisListType

P = 128
EPS = 1e-5
MASKED = -1e30
RSQRT_MAGIC = float(0x5F3759DF)
THRESH_FACTOR = 0.7

RUNS = ((0, 0, 3), (0, 1, 2), (0, 2, 1))


def wait(eng, sem, value):
    if isinstance(value, int) and value <= 0:
        return
    eng.wait_ge(sem, value)


def sandwich_block(nc, x, wqT, wkT, wvT, woT, bq, bk, bv, bo, gateT, upT, downT, gate_s, up_s, down_s, out):
    TOK, D = x.shape
    B = 2
    L = TOK // B
    H = 32
    HD = D // H
    KT = D // P
    TT = TOK // P
    LT = L // P
    HID = gateT.shape[2]
    HT = HID // P
    GH = 4
    NG = H // GH * B
    ROWS = sum(n for _, _, n in RUNS) * HD
    MROWS = ROWS + 2
    SLOTS = 4

    q_parts = nc.dram_tensor("q_parts", [H, 3 * HD, TOK], BF16, kind="Internal").ap()
    k_parts = nc.dram_tensor("k_parts", [H, 3 * HD, TOK], BF16, kind="Internal").ap()

    ctx = ExitStack()
    with ctx:
        def sb(name, shape, dt, stack=ctx):
            return stack.enter_context(nc.sbuf_tensor(name, shape, dt))

        def ps(name, shape, dt, stack):
            return stack.enter_context(nc.psum_tensor(name, shape, dt))

        def sem(name):
            return ctx.enter_context(nc.semaphore(name))

        identf = sb("identf", [P, P], F32)
        ident16 = sb("ident16", [P, P], F16)
        v_sb = sb("v_sb", [P, TT, D], F32)
        gate_t = sb("gate_t", [P, KT, HID], F16)
        up_t = sb("up_t", [P, KT, HID], F16)
        down_t16 = sb("down_t16", [P, HT, D], BF16)
        gs_n = sb("gs_n", [P, HT], F32)
        us_n = sb("us_n", [P, HT], F32)

        def rsqrt_steps(eng, link, var, y, tmp):
            w = tmp[:, 0, :]
            a = tmp[:, 1, :]
            link(eng.tensor_scalar(w, var, EPS, None, ALU.add))
            link(eng.tensor_scalar(a.bitcast(I32), w.bitcast(I32), 1, None, ALU.logical_shift_right))
            link(eng.tensor_scalar(y.bitcast(I32), a.bitcast(I32), -1.0, RSQRT_MAGIC, ALU.mult, ALU.add))
            for _ in range(4):
                link(eng.tensor_tensor(a, y, y, ALU.mult))
                link(eng.tensor_tensor(a, a, w, ALU.mult))
                link(eng.tensor_scalar(a, a, -0.5, 1.5, ALU.mult, ALU.add))
                link(eng.tensor_tensor(y, y, a, ALU.mult))

        ph = ExitStack()
        with ph:
            xs = sb("xs", [P, TT, D], F32, ph)
            xnT = sb("xnT", [P, KT, TOK], F32, ph)
            w_sb = [sb(f"w_{n}", [P, KT, D], F32, ph) for n in "qkv"]
            bq_sb = sb("bq_sb", [P, KT], F32, ph)
            bq4 = sb("bq4", [P, KT], F32, ph)
            bk_sb = sb("bk_sb", [P, KT], F32, ph)
            bv_sb = sb("bv_sb", [P, D], F32, ph)
            gs_sb = sb("gs_sb", [P, HT], F32, ph)
            us_sb = sb("us_sb", [P, HT], F32, ph)
            stats = sb("stats", [P, TT, 6], F32, ph)
            mv = sb("mv", [P, TT, 2], F32, ph)
            rstd = sb("rstd", [P, TT], F32, ph)
            rtmp = sb("rtmp", [P, 2, LT], F32, ph)
            full = sb("full", [P, 2, L], F32, ph)
            rest = sb("rest", [P, 2, L], F32, ph)
            parts = sb("parts", [P, 2, 3, L], BF16, ph)
            CH = 4
            CW = KT * HID // CH
            RAW = 6
            raw = sb("raw", [P, RAW, CW], F32, ph)
            above = sb("above", [P, 2, CW], BF16, ph)
            junk = sb("junk", [P, CW], BF16, ph)
            asum = sb("asum", [P, 3 * CH], F32, ph)
            ones = sb("ones", [P, P], F32, ph)
            tot = sb("tot", [P, 3], F32, ph)
            thr = sb("thr", [P, 3], F32, ph)
            nthr = sb("nthr", [P, 3], F32, ph)

            turned = [ps(f"turned{i}", [P, L], F32, ph) for i in range(2)]
            proj = [ps(f"proj{i}", [P, L], F32, ph) for i in range(4)]
            abs_total = ps("abs_total", [P, CH], F32, ph)

            s_x = [sem(f"x_loaded{t}") for t in range(TT)]
            s_w = [sem(f"w_loaded{n}") for n in "qkv"]
            s_small = sem("small_loaded")
            s_raw = [sem(f"raw_loaded{i}") for i in range(RAW)]
            s_ident = sem("ident_made")
            s_ones = sem("ones_made")
            s_link = sem("dve_link")
            s_bq4 = sem("bq4_made")
            s_xn = sem("x_normed")
            s_turn = sem("x_turned")
            s_xnT = sem("xnT_copied")
            s_proj = sem("proj_ready")
            s_full = sem("full_ready")
            s_hi = sem("high_ready")
            s_rest = sem("rest_ready")
            s_mid = sem("mid_ready")
            s_low = sem("low_ready")
            s_vev = sem("v_copied")
            s_parts = [sem(f"parts_stored{i}") for i in range(2)]
            s_asum = sem("abs_summed")
            s_abst = sem("abs_total_ready")
            s_thr = sem("thr_ready")
            s_above = sem("above_ready")
            s_tern = sem("ternary_ready")

            units = []
            for b in range(B):
                units += [("q", c, b) for c in range(KT)] + [("k", c, b) for c in range(KT)]
                units += [("v", b * LT + t, b) for t in range(LT)]
            qk_units = [u for u in units if u[0] != "v"]
            raw_src = [gateT, upT, downT.rearrange("p (a h) d -> p a (h d)", a=CH)]
            abs_after = {4 + int(1.4 * j): j for j in range(3 * CH)}

            block = ph.enter_context(nc.Block())

            @block.sync
            def _(sp):
                def load_x(t):
                    sp.dma_start(xs[:, t, :], x[t * P:(t + 1) * P, :]).then_inc(s_x[t], 16)

                for t in range(LT):
                    load_x(t)
                sp.dma_start(w_sb[0][:, :, :], wqT).then_inc(s_w[0], 16)
                sp.dma_start(bq_sb[:, :], bq).then_inc(s_small, 16)
                sp.dma_start(bk_sb[:, :], bk).then_inc(s_small, 16)
                sp.dma_start(bv_sb[:, :], bv).then_inc(s_small, 16)
                sp.dma_start(gs_sb[:, :], gate_s).then_inc(s_small, 16)
                sp.dma_start(us_sb[:, :], up_s).then_inc(s_small, 16)
                sp.dma_start(w_sb[1][:, :, :], wkT).then_inc(s_w[1], 16)
                for t in range(LT, TT):
                    load_x(t)
                sp.dma_start(w_sb[2][:, :, :], wvT).then_inc(s_w[2], 16)

                def load_raw(j):
                    wait(sp, s_tern, j - RAW + 1)
                    sp.dma_start(raw[:, j % RAW, :], raw_src[j // CH][:, j % CH, :]).then_inc(s_raw[j % RAW], 16)

                for j in range(RAW):
                    load_raw(j)
                later = list(range(RAW, 3 * CH))
                for n, (kind, c, b) in enumerate(qk_units):
                    sp.wait_ge(s_low, n + 1)
                    for part in range(3):
                        row = HD * (part if kind == "q" else 2 - part)
                        dst = (q_parts if kind == "q" else k_parts)[8 * c:8 * c + 8, row:row + HD, b * L:(b + 1) * L]
                        sp.dma_start(dst, parts[:, n % 2, part, :]).then_inc(s_parts[n % 2], 16)
                    if n >= 7 and later:
                        load_raw(later.pop(0))
                for j in later:
                    load_raw(j)
                for i in range(2):
                    sp.wait_ge(s_parts[i], 48 * len(qk_units) // 2)

            @block.gpsimd
            def _(pool):
                pool.memset(identf[:, :], 0.0).then_inc(s_ident, 1)
                pool.wait_ge(s_ident, 1)
                pool.affine_select(out=identf[:, :], in_=identf[:, :], compare_op=ALU.not_equal, fill=1.0,
                                   base=0, pattern=[[-1, P]], channel_multiplier=1).then_inc(s_ident, 1)
                pool.wait_ge(s_ident, 2)
                pool.tensor_copy(ident16[:, :], identf[:, :]).then_inc(s_ident, 1)
                pool.memset(ones[:, :], 1.0).then_inc(s_ones, 1)
                for j in range(3 * CH):
                    m = j // CH
                    pool.wait_ge(s_thr, m + 1)
                    wait(pool, s_tern, j - 1)
                    pool.tensor_scalar(above[:, j % 2, :], raw[:, j % RAW, :], thr[:, m:m + 1], None,
                                       ALU.is_gt).then_inc(s_above, 1)

            @block.tensor
            def _(pe):
                pe.wait_ge(s_ident, 2)
                pe.wait_ge(s_ones, 1)

                def turn(t):
                    pe.wait_ge(s_xn, t // LT * LT + t % LT + 1)
                    wait(pe, s_xnT, t - 1)
                    for k in range(KT):
                        mm = pe.transpose(turned[t % 2][:, k * P:(k + 1) * P], xs[:, t, k * P:(k + 1) * P], identf[:, :])
                    mm.then_inc(s_turn, 1)

                def threshold_sum(m):
                    pe.wait_ge(s_asum, CH * (m + 1))
                    wait(pe, s_thr, m)
                    pe.matmul(abs_total[:, :], ones[:, :], asum[:, CH * m:CH * m + CH], start=True, stop=True).then_inc(s_abst, 1)

                sums = {10: 0, 15: 1, 21: 2}
                for t in range(LT):
                    turn(t)
                for n, (kind, c, b) in enumerate(units):
                    if n == 4:
                        for t in range(LT, TT):
                            turn(t)
                    pe.wait_ge(s_w["qkv".index(kind)], 16)
                    pe.wait_ge(s_xnT, LT * (b + 1))
                    before = units[:max(n - 3, 0)]
                    wait(pe, s_full, sum(u[0] != "v" for u in before))
                    wait(pe, s_vev, sum(u[0] == "v" for u in before))
                    for k in range(KT):
                        if kind == "v":
                            mm = pe.matmul(proj[n % 4][:, :], xnT[:, k, c * P:(c + 1) * P], w_sb[2][:, k, :],
                                           start=k == 0, stop=k == KT - 1)
                        else:
                            w = w_sb["qk".index(kind)]
                            mm = pe.matmul(proj[n % 4][:, :], w[:, k, c * P:(c + 1) * P], xnT[:, k, b * L:(b + 1) * L],
                                           start=k == 0, stop=k == KT - 1)
                    mm.then_inc(s_proj, 1)
                    if n in sums:
                        threshold_sum(sums[n])

            @block.scalar
            def _(act):
                def copy_turned(t):
                    act.wait_ge(s_turn, t + 1)
                    act.activation(xnT[:, :, t * P:(t + 1) * P],
                                   turned[t % 2][:, :].rearrange("p (k t) -> p k t", k=KT), ACT.Identity).then_inc(s_xnT, 1)

                def abs_sum(j):
                    act.wait_ge(s_raw[j % RAW], 16 * (j // RAW + 1))
                    if j:
                        act.wait_ge(s_asum, j)
                    act.activation(junk[:, :], raw[:, j % RAW, :], ACT.Abs, accum_out=asum[:, j:j + 1]).then_inc(s_asum, 1)

                for t in range(LT):
                    copy_turned(t)
                q = 0
                for n, (kind, c, b) in enumerate(units):
                    if n == 2:
                        for t in range(LT, TT):
                            copy_turned(t)
                    if n == 0:
                        act.wait_ge(s_small, 80)
                        act.wait_ge(s_bq4, 1)
                    if kind != "v":
                        act.wait_ge(s_proj, n + 1)
                        wait(act, s_low, q - 1)
                        if q >= 2:
                            act.wait_ge(s_parts[q % 2], 48 * (q // 2))
                        if kind == "q":
                            act.activation(full[:, q % 2, :], proj[n % 4][:, :], ACT.Identity, bias=bq4[:, c:c + 1],
                                           scale=float(HD) ** -0.5).then_inc(s_full, 1)
                        else:
                            act.activation(full[:, q % 2, :], proj[n % 4][:, :], ACT.Identity,
                                           bias=bk_sb[:, c:c + 1]).then_inc(s_full, 1)
                        act.wait_ge(s_full, q + 1)
                        act.activation(parts[:, q % 2, 0, :], full[:, q % 2, :], ACT.Copy).then_inc(s_hi, 1)
                        act.wait_ge(s_rest, q + 1)
                        act.activation(parts[:, q % 2, 1, :], rest[:, q % 2, :], ACT.Copy).then_inc(s_mid, 1)
                        q += 1
                    if n in abs_after:
                        abs_sum(abs_after[n])

            @block.vector
            def _(dve):
                chain = [0]

                def link(ins):
                    chain[0] += 1
                    ins.then_inc(s_link, 1)
                    dve.wait_ge(s_link, chain[0])

                def norm(b):
                    for t in range(b * LT, (b + 1) * LT):
                        dve.wait_ge(s_x[t], 16)
                        link(dve.bn_stats(stats[:, t, :], xs[:, t, :]))
                        link(dve.bn_aggr(mv[:, t, :], stats[:, t, :]))
                    rsqrt_steps(dve, link, mv[:, b * LT:(b + 1) * LT, 1], rstd[:, b * LT:(b + 1) * LT], rtmp)
                    for t in range(b * LT, (b + 1) * LT):
                        dve.tensor_scalar(xs[:, t, :], xs[:, t, :], mv[:, t, 0:1], rstd[:, t:t + 1],
                                          ALU.subtract, ALU.mult).then_inc(s_xn, 1)

                def threshold(m):
                    dve.wait_ge(s_abst, m + 1)
                    link(dve.tensor_reduce(tot[:, m:m + 1], abs_total[:, :], AX.X, ALU.add))
                    link(dve.tensor_scalar(thr[:, m:m + 1], tot[:, m:m + 1], 1.0 / (P * KT * HID), THRESH_FACTOR,
                                           ALU.mult, ALU.mult))
                    dve.tensor_scalar(nthr[:, m:m + 1], thr[:, m:m + 1], -1.0, None, ALU.mult).then_inc(s_thr, 1)
                    dve.wait_ge(s_thr, m + 1)

                down_v = down_t16[:, :, :].rearrange("p (a h) d -> p a (h d)", a=CH)
                dests = [gate_t, up_t, down_v]

                def ternary(j):
                    m = j // CH
                    dve.wait_ge(s_above, j + 1)
                    dve.scalar_tensor_tensor(out=dests[m][:, j % CH, :], in0=raw[:, j % RAW, :], scalar=nthr[:, m:m + 1],
                                             in1=above[:, j % 2, :], op0=ALU.is_lt, op1=ALU.subtract).then_inc(s_tern, 1)

                norm(0)
                dve.wait_ge(s_small, 80)
                dve.tensor_scalar(bq4[:, :], bq_sb[:, :], float(HD) ** -0.5, None, ALU.mult).then_inc(s_bq4, 1)
                dve.tensor_scalar(gs_n[:, :], gs_sb[:, :], -1.0, None, ALU.mult)
                dve.tensor_scalar(us_n[:, :], us_sb[:, :], -1.0, None, ALU.mult)
                norm(1)
                work = {11: [("t", 0)], 12: [0], 13: [1], 14: [2], 15: [3], 16: [("t", 1)], 17: [4], 18: [5], 20: [6],
                        21: [7], 22: [("t", 2)], 23: [8, 9, 10, 11]}
                q = 0
                for n, (kind, c, b) in enumerate(units):
                    if kind == "v":
                        dve.wait_ge(s_proj, n + 1)
                        dve.tensor_tensor(v_sb[:, c, :], proj[n % 4][:, :], bv_sb[:, :], ALU.add).then_inc(s_vev, 1)
                    else:
                        dve.wait_ge(s_hi, q + 1)
                        dve.tensor_tensor(rest[:, q % 2, :], full[:, q % 2, :], parts[:, q % 2, 0, :],
                                          ALU.subtract).then_inc(s_rest, 1)
                        dve.wait_ge(s_mid, q + 1)
                        dve.tensor_tensor(parts[:, q % 2, 2, :], rest[:, q % 2, :], parts[:, q % 2, 1, :],
                                          ALU.subtract).then_inc(s_low, 1)
                        q += 1
                    for w in work.get(n, []):
                        if isinstance(w, tuple):
                            threshold(w[1])
                        else:
                            ternary(w)

        attn = sb("attn", [P, TT, D], F32)
        ph = ExitStack()
        with ph:
            qs = sb("qs", [P, SLOTS, GH, L], BF16, ph)
            ks = sb("ks", [P, SLOTS, GH, L], BF16, ph)
            later_keys = sb("later_keys", [P, L], F32, ph)
            tick_p = sb("tick_p", [P, 1 + LT * SLOTS], F32, ph)
            tick = sb("tick", [P, 16 * SLOTS], F32, ph)
            mx = sb("mx", [P, 2, GH * LT], F32, ph)
            nm = sb("nm", [GH * LT, 2, 2, P], BF16, ph)
            probs = [sb(f"probs{k}", [P, GH, L - k * P], F32, ph) for k in range(LT)]
            vals = sb("vals", [P, 2, LT, GH, 2 * HD], F32, ph)
            oT = sb("oT", [P, 2, L], F32, ph)
            rden = sb("rden", [P, 2, LT, GH], F32, ph)

            s1 = [ps(f"s1_{i}", [P, L], F32, ph) for i in range(2)]
            s2 = [ps(f"s2_{i}", [P, 2, L], F32, ph) for i in range(2)]
            o_ps = ps("o_ps", [P, L], F32, ph)
            misc = ps("misc", [P, L], F32, ph)

            a_load = [sem(f"parts_loaded{i}") for i in range(SLOTS)]
            a_mrow = [sem(f"max_rows_placed{i}") for i in range(SLOTS)]
            a_mask = sem("mask_made")
            a_kones = sem("key_ones_made")
            a_vones = sem("value_ones_made")
            a_s1 = sem("scores_ready")
            a_max = sem("max_done")
            a_mT = sem("max_turned")
            a_nmh = sem("neg_max_high")
            a_nml = sem("neg_max_mid")
            a_s2 = sem("shifted_scores_ready")
            a_exp = sem("exp_done")
            a_sel = sem("later_keys_cleared")
            a_vals = sem("values_gathered")
            a_pv = sem("pv_done")
            a_oev = sem("sums_copied")
            a_oT = sem("sums_turned")
            a_den = sem("denominators_inverted")
            a_norm = sem("group_normalised")

            U = SLOTS

            def steps(eng, step):
                for s in range(U):
                    step(0, s, s)
                with eng.Fori(1, NG // U) as i:
                    for s in range(U):
                        step(i, s, None)
                for s in range(3):
                    step(NG // U, s, NG + s)

            def has(n, lag):
                return n is None or 0 <= n - lag < NG

            block = ph.enter_context(nc.Block())

            @block.sync
            def _(sp):
                def load(i, s):
                    h0 = 8 * i + 4 * (s % 2)
                    t0 = (s // 2) * L
                    sl = a_load[s]

                    row = 0
                    for q0, k0, n in RUNS:
                        for dst, src, first in ((qs, q_parts, q0), (ks, k_parts, k0)):
                            rows = src[bass.ds(h0, GH), first * HD:(first + n) * HD, t0:t0 + L]
                            sp.dma_start(dst[row:row + n * HD, s, :, :], rows.rearrange("h r t -> r h t")).then_inc(sl, 16)
                        row += n * HD

                def step(i, s, n):
                    if has(n, 0):
                        wait(sp, a_s2, 8 * (U * i + s) - 24)
                        load(i, s)
                    if has(n, 2):
                        m = (s - 2) % U
                        sp.wait_ge(a_nml, U * i + s - 1)
                        for part in range(2):
                            row = qs[ROWS + part:ROWS + part + 1, m, :, :].rearrange("o h (q t) -> o (h q) t", t=P)
                            sp.dma_start(row, nm[:, s % 2, part, :]).then_inc(a_mrow[m], 16)

                steps(sp, step)

            @block.gpsimd
            def _(pool):
                pool.memset(later_keys[:, :], 0.0).then_inc(a_mask, 1)
                pool.wait_ge(a_mask, 1)
                pool.affine_select(out=later_keys[:, L - P:L], in_=later_keys[:, L - P:L], compare_op=ALU.is_ge,
                                   fill=MASKED, base=0, pattern=[[-1, P]], channel_multiplier=1).then_inc(a_mask, 1)
                pool.memset(vals[:, :, :, :, :], 1.0).then_inc(a_vones, 1)
                pool.wait_ge(a_vones, 1)
                pool.memset(tick_p[:, :], 0.0).then_inc(a_vones, 1)
                pool.wait_ge(a_vones, 2)

                def gather(i, s):
                    h0 = 8 * i + 4 * (s % 2)
                    t0 = (s // 2) * LT
                    pool.tensor_copy(vals[:, s % 2, :, :, 0:HD],
                                     v_sb[:, t0:t0 + LT, bass.ds(h0 * HD, GH * HD)].rearrange("p t (h d) -> p t h d", h=GH)
                                     ).then_inc(a_vals, 1)

                def step(i, s, n):
                    at = U * i + s
                    for k in range(LT):
                        if has(n, 2):
                            wait(pool, a_exp, 8 * (at - 2) + 2 * k + 2)
                            if n is None:
                                pool.tensor_tensor(tick_p[:, LT * s + k + 1:LT * s + k + 2], tick_p[:, 0:1], tick_p[:, 0:1], ALU.add)
                            tri = probs[k][:, :, 0:P]
                            pool.affine_select(out=tri, in_=tri, compare_op=ALU.is_ge, fill=0.0, base=0,
                                               pattern=[[0, GH], [1, P]], channel_multiplier=-1).then_inc(a_sel, 1)
                        if k == 1 and has(n, 1):
                            if has(n, 3):
                                wait(pool, a_pv, 4 * (at - 2))
                            if s == 0:
                                gather(i - 1, U - 1)
                            else:
                                gather(i, s - 1)

                steps(pool, step)

            @block.tensor
            def _(pe):
                pe.wait_ge(a_kones, SLOTS)

                def scores(i, s, j):
                    at = U * i + s
                    qt, h = LT - 1 - j // GH, j % GH
                    if j == 0:
                        pe.wait_ge(a_load[s], 96 * (i + 1))
                    wait(pe, a_max, 16 * at + j - 1)
                    pe.matmul(s1[j % 2][:, 0:(qt + 1) * P], qs[0:ROWS, s, h, qt * P:(qt + 1) * P],
                              ks[0:ROWS, s, h, 0:(qt + 1) * P], start=True, stop=True).then_inc(a_s1, 1)

                def shifted(i, s, n, k, pair):
                    at = U * i + s - 2
                    sl = (s - 2) % U
                    if k == 0 and pair == 0:
                        pe.wait_ge(a_mrow[sl], 32 * (i + 1) if s >= 2 else 32 * i)
                    wait(pe, a_exp, 8 * at + 2 * k + pair - 1)
                    for h in range(2 * pair, 2 * pair + 2):
                        mm = pe.matmul(s2[pair][:, h % 2, 0:L - k * P], ks[0:MROWS, sl, h, k * P:(k + 1) * P],
                                       qs[0:MROWS, sl, h, k * P:L], start=True, stop=True)
                    mm.then_inc(a_s2, 1)

                def products(at, par, k):
                    pe.wait_ge(a_sel, 4 * at + k + 1)
                    if k == 0:
                        pe.wait_ge(a_vals, at + 1)
                        wait(pe, a_oev, at)
                    for h in range(GH):
                        mm = pe.matmul(o_ps[2 * HD * h:2 * HD * (h + 1), k * P:L], vals[:, par, k, h, :],
                                       probs[k][:, h, :], start=k == 0, stop=k == LT - 1, skip_group_check=True)
                    mm.then_inc(a_pv, 1)

                def step(i, s, n):
                    at = U * i + s
                    for u in range(8):
                        if has(n, 0):
                            scores(i, s, 2 * u)
                            scores(i, s, 2 * u + 1)
                        if has(n, 2):
                            shifted(i, s, n, u // 2, u % 2)
                        if u == 1 and has(n, 3):
                            products(at - 3, (s - 3) % 2, 3)
                        if u == 1 and has(n, 1):
                            pe.wait_ge(a_max, 16 * at)
                            wait(pe, a_norm, at - 3)
                            pe.transpose(misc[0:GH * LT, 0:P], mx[:, (s - 1) % 2, :], identf[:, :]).then_inc(a_mT, 1)
                        if u == 4 and has(n, 3):
                            pe.wait_ge(a_oev, at - 2)
                            if has(n, 1):
                                pe.wait_ge(a_nml, at)
                            else:
                                pe.wait_ge(a_norm, at - 3)
                            for t in range(LT):
                                mm = pe.transpose(misc[:, t * P:(t + 1) * P], oT[:, (s - 3) % 2, t * P:(t + 1) * P], identf[:, :])
                            mm.then_inc(a_oT, 1)
                        if u in (3, 5, 7) and has(n, 2):
                            products(at - 2, (s - 2) % 2, (u - 3) // 2)

                steps(pe, step)

            @block.scalar
            def _(act):
                def step(i, s, n):
                    at = U * i + s
                    for u in range(8):
                        if has(n, 2):
                            k, pair = u // 2, u % 2
                            act.wait_ge(a_s2, 8 * (at - 2) + u + 1)
                            wait(act, a_pv, 4 * (at - 3) + k + 1)
                            act.activation(probs[k][:, 2 * pair:2 * pair + 2, :], s2[pair][:, :, 0:L - k * P],
                                           ACT.Exp).then_inc(a_exp, 1)
                        if u == 1 and has(n, 3):
                            act.wait_ge(a_pv, 4 * (at - 2))
                            wait(act, a_oT, at - 4)
                            act.activation(oT[:, (s - 3) % 2, :], o_ps[:, :], ACT.Copy).then_inc(a_oev, 1)
                        if u == 1 and has(n, 1):
                            act.wait_ge(a_mT, at)
                            if n is None or n >= 3:
                                sl = (s - 3) % U
                                act.wait_ge(a_mrow[sl], 32 * (i + 1) if s >= 3 else 32 * i)
                            act.activation(nm[:, (s - 1) % 2, 0, :], misc[0:GH * LT, 0:P], ACT.Copy,
                                           scale=-1.0).then_inc(a_nmh, 1)

                steps(act, step)

            @block.vector
            def _(dve):
                for s in range(SLOTS):
                    dve.memset(ks[ROWS:P, s, :, :], 1.0).then_inc(a_kones, 1)
                dve.wait_ge(a_mask, 2)

                def step(i, s, n):
                    at = U * i + s
                    for j in range(16):
                        if has(n, 0):
                            qt, h = LT - 1 - j // GH, j % GH
                            if j == 0:
                                wait(dve, a_mT, at - 1)
                            dve.wait_ge(a_s1, 16 * at + j + 1)
                            if n is None:
                                dve.memset(tick[:, 16 * s + j:16 * s + j + 1], 0.0)
                            dve.tensor_tensor_reduce(s1[j % 2][:, 0:(qt + 1) * P], s1[j % 2][:, 0:(qt + 1) * P],
                                                     later_keys[:, L - (qt + 1) * P:L], 1.0, 3.0 * MASKED, ALU.add, ALU.max,
                                                     mx[:, s % 2, h * LT + qt:h * LT + qt + 1]).then_inc(a_max, 1)
                        if j == 3 and has(n, 1):
                            dve.wait_ge(a_nmh, at)
                            dve.scalar_tensor_tensor(out=nm[:, (s - 1) % 2, 1, :], in0=misc[0:GH * LT, 0:P], scalar=-1.0,
                                                     in1=nm[:, (s - 1) % 2, 0, :], op0=ALU.mult, op1=ALU.subtract).then_inc(a_nml, 1)
                        if j == 11 and has(n, 3):
                            dve.wait_ge(a_oT, at - 2)
                            sums = misc[:, :].rearrange("p (t h e) -> p t h e", t=LT, h=GH)
                            r = rden[:, s % 2, :, :]
                            dve.reciprocal(r, sums[:, :, :, HD]).then_inc(a_den, 1)
                            dve.wait_ge(a_den, at - 2)
                            g, gi = ((s - 3) % U, i if s >= 3 else i - 1)
                            dst = attn[:, (g // 2) * LT:(g // 2 + 1) * LT, bass.ds((8 * gi + 4 * (g % 2)) * HD, GH * HD)]
                            dve.tensor_tensor(dst.rearrange("p t (h d) -> p t h d", h=GH), sums[:, :, :, 0:HD],
                                              r.unsqueeze(3).to_broadcast([P, LT, GH, HD]), ALU.mult).then_inc(a_norm, 1)

                steps(dve, step)

        ph = ExitStack()
        with ph:
            wo_sb = sb("wo_sb", [P, KT, D], F32, ph)
            bo_sb = sb("bo_sb", [P, D], F32, ph)
            ds_sb = sb("ds_sb", [P, D], F32, ph)
            ds_n = sb("ds_n", [P, D], F32, ph)
            xr = sb("xr", [P, TT, D], F32, ph)
            attnT = sb("attnT", [P, 2, KT, P], F32, ph)
            y1 = sb("y1", [P, LT, D], F32, ph)
            x2 = sb("x2", [P, 2, D], F32, ph)
            xh = sb("xh", [P, 2, 2, D], F16, ph)
            x2T = sb("x2T", [P, 2, KT, TOK], F16, ph)
            down_t = sb("down_t", [P, HT, D], F32R, ph)
            stats = sb("stats3", [P, TT, 6], F32, ph)
            mv = sb("mv3", [P, TT, 2], F32, ph)
            rstd = sb("rstd3", [P, TT], F32, ph)
            nmr = sb("nmr3", [P, TT], F32, ph)
            rtmp = sb("rtmp3", [P, 2, LT], F32, ph)
            silu = sb("silu", [P, 2, L], F32, ph)
            hid = sb("hid", [P, 2, L], F32, ph)
            hidH = sb("hidH", [P, 2, L], F32R, ph)
            hidL = sb("hidL", [P, 2, L], F32R, ph)

            c_wo = sem("wo_loaded")
            c_small = sem("small3_loaded")
            c_x = sem("x_reloaded")
            c_link = sem("dve_link3")
            c_down = sem("down_widened")
            c_aT = sem("attn_turned")
            c_aTc = sem("attnT_copied")
            c_y = sem("y_ready")
            c_y1 = sem("y1_ready")
            c_r1 = sem("rstd1_ready")
            c_n1 = sem("y_normed")
            c_x1 = sem("x1_ready")
            c_r2 = sem("rstd2_ready")
            c_n2 = sem("x1_normed")
            c_hi = sem("x2_high")
            c_lo = sem("x2_low")
            c_xT = sem("x2_turned")
            c_x2T = sem("x2T_copied")

            with ExitStack() as banks:
                aT_ps = [ps(f"aT_ps{i}", [P, KT, P], F32, banks) for i in range(2)]
                y_ps = [ps(f"y_ps{i}", [P, D], F32, banks) for i in range(2)]
                xT_ps = [ps(f"xT_ps{i}", [P, 2, KT, P], F16, banks) for i in range(2)]
                block = banks.enter_context(nc.Block())

                @block.sync
                def _(sp):
                    sp.dma_start(wo_sb[:, :, :], woT).then_inc(c_wo, 16)
                    sp.dma_start(bo_sb[:, :], bo).then_inc(c_small, 16)
                    sp.dma_start(ds_sb[:, :], down_s).then_inc(c_small, 16)
                    sp.dma_start(xr[:, :, :], x.rearrange("(t p) d -> p t d", p=P)).then_inc(c_x, 16)

                @block.gpsimd
                def _(pool):
                    for t in range(TT):
                        pool.wait_ge(c_hi, t + 1)
                        wait(pool, c_xT, t - 1)
                        pool.tensor_tensor(xh[:, t % 2, 1, :], x2[:, t % 2, :], xh[:, t % 2, 0, :], ALU.subtract).then_inc(c_lo, 1)

                @block.tensor
                def _(pe):
                    pe.wait_ge(c_wo, 16)

                    def project(t):
                        wait(pe, c_aTc, t - 1)
                        for k in range(KT):
                            mm = pe.transpose(aT_ps[t % 2][:, k, :], attn[:, t, k * P:(k + 1) * P], identf[:, :])
                        mm.then_inc(c_aT, 1)
                        pe.wait_ge(c_aTc, t + 1)
                        wait(pe, c_y1, t - 1)
                        for k in range(KT):
                            mm = pe.matmul(y_ps[t % 2][:, :], attnT[:, t % 2, k, :], wo_sb[:, k, :], start=k == 0, stop=k == KT - 1)
                        mm.then_inc(c_y, 1)

                    def turn(t):
                        pe.wait_ge(c_lo, t + 1)
                        wait(pe, c_x2T, t - 1)
                        for part in range(2):
                            for k in range(KT):
                                mm = pe.transpose(xT_ps[t % 2][:, part, k, :], xh[:, t % 2, part, k * P:(k + 1) * P], ident16[:, :])
                        mm.then_inc(c_xT, 1)

                    for t in range(LT):
                        project(t)
                    for t in range(LT, TT):
                        project(t)
                        turn(t - LT)
                    for t in range(LT, TT):
                        turn(t)

                @block.scalar
                def _(act):
                    def copy_attnT(t):
                        act.wait_ge(c_aT, t + 1)
                        wait(act, c_y, t - 1)
                        act.activation(attnT[:, t % 2, :, :], aT_ps[t % 2][:, :, :], ACT.Copy).then_inc(c_aTc, 1)

                    def norm_y(t):
                        act.wait_ge(c_r1, t // LT + 1)
                        act.activation(y1[:, t % LT, :], y1[:, t % LT, :], ACT.Identity, bias=nmr[:, t:t + 1],
                                       scale=rstd[:, t:t + 1]).then_inc(c_n1, 1)

                    def norm_x1(t):
                        act.wait_ge(c_r2, t // LT + 1)
                        wait(act, c_lo, t - 1)
                        act.activation(x2[:, t % 2, :], xr[:, t, :], ACT.Identity, bias=nmr[:, t:t + 1],
                                       scale=rstd[:, t:t + 1]).then_inc(c_n2, 1)
                        act.wait_ge(c_n2, t + 1)
                        wait(act, c_xT, t - 1)
                        act.activation(xh[:, t % 2, 0, :], x2[:, t % 2, :], ACT.Copy).then_inc(c_hi, 1)

                    def copy_x2T(t):
                        act.wait_ge(c_xT, t + 1)
                        act.activation(x2T[:, :, :, t * P:(t + 1) * P], xT_ps[t % 2][:, :, :, :], ACT.Copy).then_inc(c_x2T, 1)

                    def widen(a):
                        act.activation(down_t[:, 4 * a:4 * a + 4, :], down_t16[:, 4 * a:4 * a + 4, :], ACT.Copy).then_inc(c_down, 1)

                    for t in range(LT):
                        copy_attnT(t)
                    for t in range(LT):
                        norm_y(t)
                    for t in range(LT):
                        copy_attnT(LT + t)
                        norm_x1(t)
                        if t >= 1:
                            copy_x2T(t - 1)
                    copy_x2T(LT - 1)
                    widen(0)
                    widen(1)
                    for t in range(LT, TT):
                        norm_y(t)
                    for t in range(LT, TT):
                        norm_x1(t)
                        if t > LT:
                            copy_x2T(t - 1)
                    copy_x2T(TT - 1)
                    widen(2)
                    widen(3)

                @block.vector
                def _(dve):
                    chain = [0]

                    def link(ins):
                        chain[0] += 1
                        ins.then_inc(c_link, 1)
                        dve.wait_ge(c_link, chain[0])

                    dve.wait_ge(c_small, 32)
                    link(dve.tensor_scalar(ds_n[:, :], ds_sb[:, :], -1.0, None, ALU.mult))

                    def means(b, src, done):
                        ts = slice(b * LT, (b + 1) * LT)
                        for t in range(b * LT, (b + 1) * LT):
                            link(dve.bn_stats(stats[:, t, :], src(t)))
                            link(dve.bn_aggr(mv[:, t, :], stats[:, t, :]))
                        rsqrt_steps(dve, link, mv[:, ts, 1], rstd[:, ts], rtmp)
                        dve.scalar_tensor_tensor(out=nmr[:, ts], in0=mv[:, ts, 0], scalar=-1.0, in1=rstd[:, ts],
                                                 op0=ALU.mult, op1=ALU.mult).then_inc(done, 1)

                    for b in range(B):
                        for t in range(b * LT, (b + 1) * LT):
                            dve.wait_ge(c_y, t + 1)
                            wait(dve, c_x1, t - LT + 1)
                            dve.tensor_tensor(y1[:, t % LT, :], y_ps[t % 2][:, :], bo_sb[:, :], ALU.add).then_inc(c_y1, 1)
                            dve.wait_ge(c_y1, t + 1)
                        if b:
                            dve.wait_ge(c_n2, LT)
                        means(b, lambda t: y1[:, t % LT, :], c_r1)
                        dve.wait_ge(c_x, 16)
                        for t in range(b * LT, (b + 1) * LT):
                            dve.wait_ge(c_n1, t + 1)
                            dve.tensor_tensor(xr[:, t, :], xr[:, t, :], y1[:, t % LT, :], ALU.add).then_inc(c_x1, 1)
                            dve.wait_ge(c_x1, t + 1)
                        means(b, lambda t: xr[:, t, :], c_r2)

            y_ps = [ps(f"down_ps{i}", [P, D], F32, ph) for i in range(LT)]
            g_ps = [ps(f"gate_ps{i}", [P, L], F32, ph) for i in range(2)]
            u_ps = [ps(f"up_ps{i}", [P, L], F32, ph) for i in range(2)]
            f_g = sem("gate_ready")
            f_u = sem("up_ready")
            f_silu = sem("silu_done")
            f_h = sem("hidden_ready")
            f_hh = sem("hidden_high")
            f_hl = sem("hidden_low")
            f_d = sem("down_used_hidden")
            f_y = sem("down_done")
            f_ys = sem("down_scaled")
            f_link = sem("dve_link4")
            f_r = sem("rstd_ready")
            f_n = sem("final_normed")
            f_o = sem("out_ready")
            f_st = sem("out_stored")
            block = ph.enter_context(nc.Block())

            def hidden_steps(eng, step):
                for b in range(B):
                    step(b, b * HT, 0, 0, 0)
                    step(b, b * HT + 1, 1, 1, 1)
                    with eng.Fori(1, HT // 2) as i:
                        for a in range(2):
                            step(b, b * HT + 2 * i + a, 2 * i + a, a, None)
                    step(b, (b + 1) * HT, None, 0, HT)

            @block.tensor
            def _(pe):
                def down(b, n, ht, a, first, last):
                    pe.wait_ge(f_hl, n + 1)
                    if first:
                        wait(pe, f_ys, LT * b)
                    for t in range(LT):
                        for p, part in enumerate((hidH, hidL)):
                            mm = pe.matmul(y_ps[t][:, :], part[:, a, t * P:(t + 1) * P], down_t[:, ht, :],
                                           start=first and p == 0, stop=last and p == 1)
                        if last:
                            mm.then_inc(f_y, 1)
                    if not last:
                        mm.then_inc(f_d, 1)

                def step(b, n, ht, a, k):
                    if ht is not None:
                        for w, banks, ready, free in ((gate_t, g_ps, f_g, f_silu), (up_t, u_ps, f_u, f_h)):
                            wait(pe, free, n - 1)
                            for kt in range(KT):
                                for part in range(2):
                                    mm = pe.matmul(banks[a][:, :], w[:, kt, bass.ds(ht * P, P)],
                                                   x2T[:, part, kt, b * L:(b + 1) * L],
                                                   start=kt == 0 and part == 0, stop=kt == KT - 1 and part == 1)
                            mm.then_inc(ready, 1)
                    if k != 0:
                        down(b, n - 1, HT - 1 if ht is None else ht - 1, 1 - a, k == 1, k == HT)

                hidden_steps(pe, step)

            @block.scalar
            def _(act):
                def step(b, n, ht, a, k):
                    if ht is not None:
                        act.wait_ge(f_g, n + 1)
                        wait(act, f_h, n - 1)
                        act.activation(silu[:, a, :], g_ps[a][:, :], ACT.Silu, scale=gs_n[:, bass.ds(ht, 1)]).then_inc(f_silu, 1)
                        act.wait_ge(f_h, n + 1)
                        wait(act, f_d, n - 1 - b)
                        if b and k in (0, 1):
                            act.wait_ge(f_y, LT * b)
                        act.activation(hidH[:, a, :], hid[:, a, :], ACT.Copy).then_inc(f_hh, 1)
                    if b and k == 1:
                        norm(0)

                def norm(b):
                    act.wait_ge(f_r, b + 1)
                    for t in range(LT):
                        act.activation(y1[:, t, :], y1[:, t, :], ACT.Identity, bias=nmr[:, b * LT + t:b * LT + t + 1],
                                       scale=rstd[:, b * LT + t:b * LT + t + 1]).then_inc(f_n, 1)

                hidden_steps(act, step)
                norm(1)

            @block.vector
            def _(dve):
                chain = [0]

                def link(ins):
                    chain[0] += 1
                    ins.then_inc(f_link, 1)
                    dve.wait_ge(f_link, chain[0])

                def finish(b):
                    ts = slice(b * LT, (b + 1) * LT)
                    for t in range(LT):
                        dve.wait_ge(f_y, b * LT + t + 1)
                        wait(dve, f_o, (b - 1) * LT + t + 1)
                        dve.tensor_tensor(y1[:, t, :], y_ps[t][:, :], ds_n[:, :], ALU.mult).then_inc(f_ys, 1)
                    for t in range(LT):
                        dve.wait_ge(f_ys, b * LT + t + 1)
                        link(dve.bn_stats(stats[:, b * LT + t, :], y1[:, t, :]))
                        link(dve.bn_aggr(mv[:, b * LT + t, :], stats[:, b * LT + t, :]))
                    rsqrt_steps(dve, link, mv[:, ts, 1], rstd[:, ts], rtmp)
                    dve.scalar_tensor_tensor(out=nmr[:, ts], in0=mv[:, ts, 0], scalar=-1.0, in1=rstd[:, ts],
                                             op0=ALU.mult, op1=ALU.mult).then_inc(f_r, 1)

                def add(b):
                    for t in range(LT):
                        dve.wait_ge(f_n, b * LT + t + 1)
                        dve.tensor_tensor(xr[:, b * LT + t, :], xr[:, b * LT + t, :], y1[:, t, :], ALU.add).then_inc(f_o, 1)

                def step(b, n, ht, a, k):
                    if ht is not None:
                        dve.wait_ge(f_u, n + 1)
                        dve.wait_ge(f_silu, n + 1)
                        wait(dve, f_hl, n - 1)
                        dve.scalar_tensor_tensor(out=hid[:, a, :], in0=u_ps[a][:, :], scalar=us_n[:, bass.ds(ht, 1)],
                                                 in1=silu[:, a, :], op0=ALU.mult, op1=ALU.mult).then_inc(f_h, 1)
                        dve.wait_ge(f_hh, n + 1)
                        dve.tensor_tensor(hidL[:, a, :], hid[:, a, :], hidH[:, a, :].bitcast(F32), ALU.subtract).then_inc(f_hl, 1)
                    if k == HT:
                        finish(b)
                    if b and k == 1:
                        add(0)

                hidden_steps(dve, step)
                add(1)

            @block.sync
            def _(sp):
                for t in range(TT):
                    sp.wait_ge(f_o, t + 1)
                    sp.dma_start(out[t * P:(t + 1) * P, :], xr[:, t, :]).then_inc(f_st, 16)
                sp.wait_ge(f_st, 16 * TT)


def kernel(L0_attn_x, L0_attn_Wq, L0_attn_bq, L0_attn_Wk, L0_attn_bk, L0_attn_Wv, L0_attn_bv, L0_attn_Wo, L0_attn_bo,
           L0_ffn_gate_w, L0_ffn_gate_scale, L0_ffn_up_w, L0_ffn_up_scale, L0_ffn_down_w, L0_ffn_down_scale):
    import numpy as np
    import concourse.bacc as bacc
    from concourse.bass_utils import run_bass_kernel_spmd

    D = L0_attn_x.shape[-1]

    def turned(w):
        wt = np.asarray(w).T
        return np.ascontiguousarray(wt.reshape(-1, P, wt.shape[1]).transpose(1, 0, 2))

    def columns(v):
        return np.ascontiguousarray(np.asarray(v).reshape(-1, P).T)

    def spread(v):
        return np.ascontiguousarray(np.broadcast_to(np.asarray(v).reshape(1, -1), (P, v.size)))

    arrays = {
        "x": np.ascontiguousarray(np.asarray(L0_attn_x).reshape(-1, D)),
        "wqT": turned(L0_attn_Wq), "wkT": turned(L0_attn_Wk), "wvT": turned(L0_attn_Wv), "woT": turned(L0_attn_Wo),
        "bq": columns(L0_attn_bq), "bk": columns(L0_attn_bk), "bv": spread(L0_attn_bv), "bo": spread(L0_attn_bo),
        "gateT": turned(L0_ffn_gate_w), "upT": turned(L0_ffn_up_w), "downT": turned(L0_ffn_down_w),
        "gate_s": columns(L0_ffn_gate_scale), "up_s": columns(L0_ffn_up_scale), "down_s": spread(L0_ffn_down_scale),
    }
    nc = bacc.Bacc("TRN2", target_bir_lowering=False, num_devices=1)
    args = [nc.dram_tensor(f"in_{n}", a.shape, mybir.dt.from_np(a.dtype), kind="ExternalInput").ap() for n, a in arrays.items()]
    out = nc.dram_tensor("out_0", arrays["x"].shape, F32, kind="ExternalOutput").ap()
    sandwich_block(nc, *args, out)
    r = run_bass_kernel_spmd(nc, [{f"in_{n}": a for n, a in arrays.items()}], core_ids=[0])
    return r.results[0]["out_0"].reshape(np.asarray(L0_attn_x).shape)
```

```python
from contextlib import ExitStack

import concourse.bass as bass
from concourse import mybir

F32 = mybir.dt.float32
F32R = mybir.dt.float32r
BF16 = mybir.dt.bfloat16
F16 = mybir.dt.float16
I32 = mybir.dt.int32
ALU = mybir.AluOpType
ACT = mybir.ActivationFunctionType
AX = mybir.AxisListType

P = 128
EPS = 1e-5
MASKED = -1e30
RSQRT_MAGIC = float(0x5F3759DF)
THRESH_FACTOR = 0.7

RUNS = ((0, 0, 3), (0, 1, 2), (0, 2, 1))


def wait(eng, sem, value):
    if isinstance(value, int) and value <= 0:
        return
    eng.wait_ge(sem, value)


def sandwich_block(nc, x, wqT, wkT, wvT, woT, bq, bk, bv, bo, gateT, upT, downT, gate_s, up_s, down_s, out):
    TOK, D = x.shape
    B = 2
    L = TOK // B
    H = 32
    HD = D // H
    KT = D // P
    TT = TOK // P
    LT = L // P
    HID = gateT.shape[2]
    HT = HID // P
    GH = 4
    NG = H // GH * B
    ROWS = sum(n for _, _, n in RUNS) * HD
    MROWS = ROWS + 2
    SLOTS = 4

    q_parts = nc.dram_tensor("q_parts", [H, 3 * HD, TOK], BF16, kind="Internal").ap()
    k_parts = nc.dram_tensor("k_parts", [H, 3 * HD, TOK], BF16, kind="Internal").ap()

    ctx = ExitStack()
    with ctx:
        def sb(name, shape, dt, stack=ctx):
            return stack.enter_context(nc.sbuf_tensor(name, shape, dt))

        def ps(name, shape, dt, stack):
            return stack.enter_context(nc.psum_tensor(name, shape, dt))

        def sem(name):
            return ctx.enter_context(nc.semaphore(name))

        identf = sb("identf", [P, P], F32)
        ident16 = sb("ident16", [P, P], F16)
        identb = sb("identb", [P, P], BF16)
        later_keys = sb("later_keys", [P, GH, P], BF16)
        v_sb = sb("v_sb", [P, TT, D], F32)
        gate_t = sb("gate_t", [P, KT, HID], F16)
        up_t = sb("up_t", [P, KT, HID], F16)
        down_t16 = sb("down_t16", [P, HT, D], BF16)
        gs_n = sb("gs_n", [P, HT], F32)
        us_n = sb("us_n", [P, HT], F32)

        def rsqrt_steps(eng, link, var, y, tmp):
            w = tmp[:, 0, :]
            a = tmp[:, 1, :]
            link(eng.tensor_scalar(w, var, EPS, None, ALU.add))
            link(eng.tensor_scalar(a.bitcast(I32), w.bitcast(I32), 1, None, ALU.logical_shift_right))
            link(eng.tensor_scalar(y.bitcast(I32), a.bitcast(I32), -1.0, RSQRT_MAGIC, ALU.mult, ALU.add))
            for _ in range(3):
                link(eng.tensor_tensor(a, y, w, ALU.mult))
                link(eng.scalar_tensor_tensor(out=a, in0=a, scalar=-0.5, in1=y, op0=ALU.mult, op1=ALU.mult))
                link(eng.scalar_tensor_tensor(out=y, in0=a, scalar=1.5, in1=y, op0=ALU.add, op1=ALU.mult))

        ph = ExitStack()
        with ph:
            xs = sb("xs", [P, TT, D], F32, ph)
            xnT = sb("xnT", [P, KT, TOK], F32, ph)
            w_sb = [sb(f"w_{n}", [P, KT, D], F32, ph) for n in "qkv"]
            bq_sb = sb("bq_sb", [P, KT], F32, ph)
            bk_sb = sb("bk_sb", [P, KT], F32, ph)
            bv_sb = sb("bv_sb", [P, D], F32, ph)
            gs_sb = sb("gs_sb", [P, HT], F32, ph)
            us_sb = sb("us_sb", [P, HT], F32, ph)
            stats = sb("stats", [P, TT, 6], F32, ph)
            mv = sb("mv", [P, TT, 2], F32, ph)
            rstd = sb("rstd", [P, TT], F32, ph)
            rtmp = sb("rtmp", [P, 2, LT], F32, ph)
            rest = sb("rest", [P, 2, L], F32, ph)
            PB = 3
            parts = sb("parts", [P, PB, 3, L], BF16, ph)
            CH = 4
            CW = KT * HID // CH
            RAW = 7
            raw = sb("raw", [P, RAW, CW], F32, ph)
            above = sb("above", [P, 2, CW], BF16, ph)
            junk = sb("junk", [P, CW], BF16, ph)
            asum = sb("asum", [P, 3 * CH], F32, ph)
            ones = sb("ones", [P, P], F32, ph)
            tot = sb("tot", [P, 3], F32, ph)
            thr = sb("thr", [P, 3], F32, ph)
            nthr = sb("nthr", [P, 3], F32, ph)

            turned = [ps(f"turned{i}", [P, L], F32, ph) for i in range(2)]
            proj = [ps(f"proj{i}", [P, L], F32, ph) for i in range(4)]
            abs_total = ps("abs_total", [P, CH], F32, ph)

            s_x = [sem(f"x_loaded{t}") for t in range(TT)]
            s_w = [sem(f"w_loaded{n}") for n in "qkv"]
            s_small = sem("small_loaded")
            s_raw = [sem(f"raw_loaded{i}") for i in range(RAW)]
            s_ident = sem("ident_made")
            s_ones = sem("ones_made")
            s_mask = sem("mask_made")
            s_link = sem("dve_link")
            s_xn = sem("x_normed")
            s_turn = sem("x_turned")
            s_xnT = sem("xnT_copied")
            s_proj = sem("proj_ready")
            s_hi = sem("high_ready")
            s_rest = sem("rest_ready")
            s_mid = sem("mid_ready")
            s_low = sem("low_ready")
            s_vev = sem("v_copied")
            s_parts = [sem(f"parts_stored{i}") for i in range(PB)]
            s_asum = sem("abs_summed")
            s_abst = sem("abs_total_ready")
            s_thr = sem("thr_ready")
            s_above = sem("above_ready_even")
            s_above_p = sem("above_ready_odd")
            s_tern = sem("ternary_ready")

            units = []
            for b in range(B):
                units += [("q", c, b) for c in range(KT)] + [("k", c, b) for c in range(KT)]
                units += [("v", b * LT + t, b) for t in range(LT)]
            qk_units = [u for u in units if u[0] != "v"]
            raw_src = [gateT, upT, downT.rearrange("p (a h) d -> p a (h d)", a=CH)]
            abs_after = {n: j for j, n in enumerate((1, 2, 3, 4, 5, 6, 7, 9, 10, 11, 12, 14))}

            block = ph.enter_context(nc.Block())

            @block.sync
            def _(sp):
                def load_x(t):
                    sp.dma_start(xs[:, t, :], x[t * P:(t + 1) * P, :]).then_inc(s_x[t], 16)

                for t in range(LT):
                    load_x(t)
                sp.dma_start(w_sb[0][:, :, :], wqT).then_inc(s_w[0], 16)
                sp.dma_start(bq_sb[:, :], bq).then_inc(s_small, 16)
                sp.dma_start(bk_sb[:, :], bk).then_inc(s_small, 16)
                sp.dma_start(bv_sb[:, :], bv).then_inc(s_small, 16)
                sp.dma_start(gs_sb[:, :], gate_s).then_inc(s_small, 16)
                sp.dma_start(us_sb[:, :], up_s).then_inc(s_small, 16)
                sp.dma_start(w_sb[1][:, :, :], wkT).then_inc(s_w[1], 16)
                for t in range(LT, TT):
                    load_x(t)
                sp.dma_start(w_sb[2][:, :, :], wvT).then_inc(s_w[2], 16)

                def load_raw(j):
                    wait(sp, s_tern, j - RAW + 1)
                    sp.dma_start(raw[:, j % RAW, :], raw_src[j // CH][:, j % CH, :]).then_inc(s_raw[j % RAW], 16)

                for j in range(RAW):
                    load_raw(j)
                for n, (kind, c, b) in enumerate(qk_units):
                    sp.wait_ge(s_low, n + 1)
                    for part in range(3):
                        row = HD * (part if kind == "q" else 2 - part)
                        dst = (q_parts if kind == "q" else k_parts)[8 * c:8 * c + 8, row:row + HD, b * L:(b + 1) * L]
                        sp.dma_start(dst, parts[:, n % PB, part, :]).then_inc(s_parts[n % PB], 16)
                    if n == 6:
                        load_raw(RAW)
                    if n == 7:
                        for j in range(RAW + 1, 3 * CH):
                            load_raw(j)
                for i in range(PB):
                    sp.wait_ge(s_parts[i], 48 * len(qk_units[i::PB]))

            @block.gpsimd
            def _(pool):
                pool.memset(identf[:, :], 0.0).then_inc(s_ident, 1)
                pool.wait_ge(s_ident, 1)
                pool.affine_select(out=identf[:, :], in_=identf[:, :], compare_op=ALU.not_equal, fill=1.0,
                                   base=0, pattern=[[-1, P]], channel_multiplier=1).then_inc(s_ident, 1)
                pool.wait_ge(s_ident, 2)
                pool.tensor_copy(ident16[:, :], identf[:, :]).then_inc(s_ident, 1)
                pool.tensor_copy(identb[:, :], identf[:, :]).then_inc(s_ident, 1)
                pool.memset(ones[:, :], 1.0).then_inc(s_ones, 1)
                pool.memset(later_keys[:, :, :], 0.0).then_inc(s_mask, 1)
                pool.wait_ge(s_mask, 1)
                pool.affine_select(out=later_keys[:, :, :], in_=later_keys[:, :, :], compare_op=ALU.is_ge, fill=MASKED,
                                   base=0, pattern=[[0, GH], [-1, P]], channel_multiplier=1).then_inc(s_mask, 1)
                for j in range(1, 3 * CH, 2):
                    m = j // CH
                    pool.wait_ge(s_thr, m + 1)
                    wait(pool, s_tern, j - 1)
                    pool.tensor_scalar(above[:, 1, :], raw[:, j % RAW, :], thr[:, m:m + 1], None, ALU.is_gt).then_inc(s_above_p, 1)

            @block.tensor
            def _(pe):
                pe.wait_ge(s_ident, 2)
                pe.wait_ge(s_ones, 1)

                def turn(t):
                    pe.wait_ge(s_xn, t // LT * LT + t % LT + 1)
                    wait(pe, s_xnT, t - 1)
                    for k in range(KT):
                        mm = pe.transpose(turned[t % 2][:, k * P:(k + 1) * P], xs[:, t, k * P:(k + 1) * P], identf[:, :])
                    mm.then_inc(s_turn, 1)

                def threshold_sum(m):
                    pe.wait_ge(s_asum, CH * (m + 1))
                    wait(pe, s_thr, m)
                    pe.matmul(abs_total[:, :], ones[:, :], asum[:, CH * m:CH * m + CH], start=True, stop=True).then_inc(s_abst, 1)

                sums = {6: 0, 11: 1, 16: 2}
                for t in range(LT):
                    turn(t)
                for n, (kind, c, b) in enumerate(units):
                    if n == 4:
                        for t in range(LT, TT):
                            turn(t)
                    pe.wait_ge(s_w["qkv".index(kind)], 16)
                    pe.wait_ge(s_xnT, LT * (b + 1))
                    before = units[:max(n - 3, 0)]
                    wait(pe, s_rest, sum(u[0] != "v" for u in before))
                    wait(pe, s_vev, sum(u[0] == "v" for u in before))
                    for k in range(KT):
                        if kind == "v":
                            mm = pe.matmul(proj[n % 4][:, :], xnT[:, k, c * P:(c + 1) * P], w_sb[2][:, k, :],
                                           start=k == 0, stop=k == KT - 1)
                        else:
                            w = w_sb["qk".index(kind)]
                            mm = pe.matmul(proj[n % 4][:, :], w[:, k, c * P:(c + 1) * P], xnT[:, k, b * L:(b + 1) * L],
                                           start=k == 0, stop=k == KT - 1)
                    mm.then_inc(s_proj, 1)
                    if n in sums:
                        threshold_sum(sums[n])

            @block.scalar
            def _(act):
                def copy_turned(t):
                    act.wait_ge(s_turn, t + 1)
                    act.activation(xnT[:, :, t * P:(t + 1) * P],
                                   turned[t % 2][:, :].rearrange("p (k t) -> p k t", k=KT), ACT.Identity).then_inc(s_xnT, 1)

                def abs_sum(j):
                    act.wait_ge(s_raw[j % RAW], 16 * (j // RAW + 1))
                    if j:
                        act.wait_ge(s_asum, j)
                    act.activation(junk[:, :], raw[:, j % RAW, :], ACT.Abs, accum_out=asum[:, j:j + 1]).then_inc(s_asum, 1)

                for t in range(LT):
                    copy_turned(t)
                def high_part(n, q, kind, c):
                    act.wait_ge(s_proj, n + 1)
                    wait(act, s_parts[q % PB], 48 * (q // PB))
                    bias = bq_sb if kind == "q" else bk_sb
                    act.activation(parts[:, q % PB, 0, :], proj[n % 4][:, :], ACT.Identity,
                                   bias=bias[:, c:c + 1]).then_inc(s_hi, 1)

                def mid_part(q):
                    act.wait_ge(s_rest, q + 1)
                    act.activation(parts[:, q % PB, 1, :], rest[:, q % 2, :], ACT.Copy).then_inc(s_mid, 1)

                act.wait_ge(s_small, 80)
                q = 0
                for n, (kind, c, b) in enumerate(units):
                    if n == 2:
                        for t in range(LT, TT):
                            copy_turned(t)
                    if kind != "v":
                        high_part(n, q, kind, c)
                        if units[n - 1][0] != "v" and q:
                            mid_part(q - 1)
                        q += 1
                    elif c % LT == 0:
                        mid_part(q - 1)
                    if n in abs_after:
                        abs_sum(abs_after[n])

            @block.vector
            def _(dve):
                chain = [0]

                def link(ins):
                    chain[0] += 1
                    ins.then_inc(s_link, 1)
                    dve.wait_ge(s_link, chain[0])

                def norm(b):
                    for t in range(b * LT, (b + 1) * LT):
                        dve.wait_ge(s_x[t], 16)
                        link(dve.bn_stats(stats[:, t, :], xs[:, t, :]))
                        link(dve.bn_aggr(mv[:, t, :], stats[:, t, :]))
                    rsqrt_steps(dve, link, mv[:, b * LT:(b + 1) * LT, 1], rstd[:, b * LT:(b + 1) * LT], rtmp)
                    for t in range(b * LT, (b + 1) * LT):
                        dve.tensor_scalar(xs[:, t, :], xs[:, t, :], mv[:, t, 0:1], rstd[:, t:t + 1],
                                          ALU.subtract, ALU.mult).then_inc(s_xn, 1)

                def threshold(m):
                    dve.wait_ge(s_abst, m + 1)
                    link(dve.tensor_reduce(tot[:, m:m + 1], abs_total[:, :], AX.X, ALU.add))
                    link(dve.tensor_scalar(thr[:, m:m + 1], tot[:, m:m + 1], 1.0 / (P * KT * HID), THRESH_FACTOR,
                                           ALU.mult, ALU.mult))
                    dve.tensor_scalar(nthr[:, m:m + 1], thr[:, m:m + 1], -1.0, None, ALU.mult).then_inc(s_thr, 1)
                    dve.wait_ge(s_thr, m + 1)

                down_v = down_t16[:, :, :].rearrange("p (a h) d -> p a (h d)", a=CH)
                dests = [gate_t, up_t, down_v]

                def ternary(j):
                    m = j // CH
                    if j % 2:
                        dve.wait_ge(s_above_p, j // 2 + 1)
                    else:
                        wait(dve, s_tern, j - 1)
                        dve.tensor_scalar(above[:, 0, :], raw[:, j % RAW, :], thr[:, m:m + 1], None, ALU.is_gt).then_inc(s_above, 1)
                        dve.wait_ge(s_above, j // 2 + 1)
                    dve.scalar_tensor_tensor(out=dests[m][:, j % CH, :], in0=raw[:, j % RAW, :], scalar=nthr[:, m:m + 1],
                                             in1=above[:, j % 2, :], op0=ALU.is_lt, op1=ALU.subtract).then_inc(s_tern, 1)

                norm(0)
                dve.wait_ge(s_small, 80)
                dve.tensor_scalar(gs_n[:, :], gs_sb[:, :], -1.0, None, ALU.mult)
                dve.tensor_scalar(us_n[:, :], us_sb[:, :], -1.0, None, ALU.mult)
                norm(1)
                work = {6: [("t", 0)], 7: [0], 8: [1], 9: [2], 10: [3], 12: [("t", 1), 4], 13: [5], 14: [6], 15: [7],
                        17: [("t", 2), 8], 18: [9], 19: [10], 20: [11]}

                def rest_part(n, q, kind, c):
                    dve.wait_ge(s_hi, q + 1)
                    wait(dve, s_low, q - 1)
                    bias = bq_sb if kind == "q" else bk_sb
                    dve.scalar_tensor_tensor(out=rest[:, q % 2, :], in0=proj[n % 4][:, :], scalar=bias[:, c:c + 1],
                                             in1=parts[:, q % PB, 0, :], op0=ALU.add, op1=ALU.subtract).then_inc(s_rest, 1)

                def low_part(q):
                    dve.wait_ge(s_mid, q + 1)
                    dve.tensor_tensor(parts[:, q % PB, 2, :], rest[:, q % 2, :], parts[:, q % PB, 1, :],
                                      ALU.subtract).then_inc(s_low, 1)

                q = 0
                for n, (kind, c, b) in enumerate(units):
                    if kind == "v":
                        if c % LT == 0:
                            low_part(q - 1)
                        dve.wait_ge(s_proj, n + 1)
                        dve.tensor_tensor(v_sb[:, c, :], proj[n % 4][:, :], bv_sb[:, :], ALU.add).then_inc(s_vev, 1)
                    else:
                        rest_part(n, q, kind, c)
                        if units[n - 1][0] != "v" and q:
                            low_part(q - 1)
                        q += 1
                    for w in work.get(n, []):
                        if isinstance(w, tuple):
                            threshold(w[1])
                        else:
                            ternary(w)

        attn = sb("attn", [P, TT, D], F32)
        wo_sb = sb("wo_sb", [P, KT, D], F32)
        bo_sb = sb("bo_sb", [P, D], F32)
        ds_sb = sb("ds_sb", [P, D], F32)
        xr = sb("xr", [P, TT, D], F32)
        c_wo = sem("wo_loaded")
        c_small = sem("small3_loaded")
        c_x = sem("x_reloaded")
        ph = ExitStack()
        with ph:
            qs = sb("qs", [P, SLOTS, GH, L], BF16, ph)
            ks = sb("ks", [P, SLOTS, GH, L], BF16, ph)
            tick_p = sb("tick_p", [P, 1 + LT * SLOTS], F32, ph)
            mx = sb("mx", [P, 2, GH * LT], F32, ph)
            nm = sb("nm", [GH * LT, 2, 2, P], BF16, ph)
            probs = [sb(f"probs{k}", [P, GH, L - k * P], F32, ph) for k in range(LT)]
            vals = sb("vals", [P, 2, LT, GH, 2 * HD], F32, ph)
            oT = sb("oT", [P, 2, L], F32, ph)
            rden = sb("rden", [P, 2, LT, GH], F32, ph)

            s1 = [ps(f"s1_{i}", [P, L], F32, ph) for i in range(3)]
            s2 = [ps(f"s2_{i}", [P, L], F32, ph) for i in range(3)]
            o_ps = ps("o_ps", [P, L], F32, ph)
            misc = ps("misc", [P, L], F32, ph)

            a_load = [sem(f"parts_loaded{i}") for i in range(SLOTS)]
            a_mrow = [sem(f"max_rows_placed{i}") for i in range(SLOTS)]
            a_kones = sem("key_ones_made")
            a_vones = sem("value_ones_made")
            a_s1 = sem("scores_ready")
            a_max = sem("max_done")
            a_mT = sem("max_turned")
            a_nmh = sem("neg_max_high")
            a_nml = sem("neg_max_mid")
            a_s2 = sem("shifted_scores_ready")
            a_exp = sem("exp_done")
            a_sel = sem("later_keys_cleared")
            a_vals = sem("values_gathered")
            a_pv = sem("pv_done")
            a_oev = sem("sums_copied")
            a_oT = sem("sums_turned")
            a_den = sem("denominators_inverted")
            a_norm = sem("group_normalised")

            fills = []
            for r in range(LT, 0, -1):
                heads = 1 << ((LT // r).bit_length() - 1)
                fills += [(r, h, heads) for h in range(0, GH, heads)]
            F = len(fills)
            BANKS = 3
            done_fills = [sum(f[0] >= LT - k for f in fills) for k in range(LT)]

            def bank_free(at, u):
                last = max((v for v in range(F) if v % BANKS == u % BANKS), default=0)
                return F * at + u - BANKS + 1 if u >= BANKS else F * (at - 1) + last + 1

            U = SLOTS

            def steps(eng, step):
                for s in range(U):
                    step(0, s, s)
                with eng.Fori(1, NG // U) as i:
                    for s in range(U):
                        step(i, s, None)
                for s in range(3):
                    step(NG // U, s, NG + s)

            def has(n, lag):
                return n is None or 0 <= n - lag < NG

            block = ph.enter_context(nc.Block())

            @block.sync
            def _(sp):
                def load(i, s):
                    h0 = 8 * i + 4 * (s % 2)
                    t0 = (s // 2) * L
                    sl = a_load[s]

                    row = 0
                    for q0, k0, n in RUNS:
                        for dst, src, first in ((qs, q_parts, q0), (ks, k_parts, k0)):
                            rows = src[bass.ds(h0, GH), first * HD:(first + n) * HD, t0:t0 + L]
                            sp.dma_start(dst[row:row + n * HD, s, :, :], rows.rearrange("h r t -> r h t")).then_inc(sl, 16)
                        row += n * HD

                def step(i, s, n):
                    if has(n, 0):
                        wait(sp, a_s2, F * (U * i + s - 3))
                        load(i, s)
                    if has(n, 2):
                        m = (s - 2) % U
                        sp.wait_ge(a_nml, U * i + s - 1)
                        for part in range(2):
                            row = qs[ROWS + part:ROWS + part + 1, m, :, :].rearrange("o h (q t) -> o (h q) t", t=P)
                            sp.dma_start(row, nm[:, s % 2, part, :]).then_inc(a_mrow[m], 16)
                    if n == NG + 1:
                        sp.dma_start(wo_sb[:, :, :], woT).then_inc(c_wo, 16)
                        sp.dma_start(bo_sb[:, :], bo).then_inc(c_small, 16)
                        sp.dma_start(ds_sb[:, :], down_s).then_inc(c_small, 16)
                        sp.dma_start(xr[:, :, :], x.rearrange("(t p) d -> p t d", p=P)).then_inc(c_x, 16)

                steps(sp, step)

            @block.gpsimd
            def _(pool):
                pool.memset(vals[:, :, :, :, :], 1.0).then_inc(a_vones, 1)
                pool.wait_ge(a_vones, 1)
                pool.memset(tick_p[:, :], 0.0).then_inc(a_vones, 1)
                pool.wait_ge(a_vones, 2)
                for s in range(SLOTS):
                    pool.memset(ks[ROWS:P, s, :, :], 1.0).then_inc(a_kones, 1)
                    pool.wait_ge(a_kones, s + 1)

                def gather(i, s):
                    h0 = 8 * i + 4 * (s % 2)
                    t0 = (s // 2) * LT
                    pool.tensor_copy(vals[:, s % 2, :, :, 0:HD],
                                     v_sb[:, t0:t0 + LT, bass.ds(h0 * HD, GH * HD)].rearrange("p t (h d) -> p t h d", h=GH)
                                     ).then_inc(a_vals, 1)

                def step(i, s, n):
                    at = U * i + s
                    for k in range(LT):
                        if has(n, 2):
                            wait(pool, a_exp, F * (at - 2) + done_fills[k])
                            if n is None:
                                pool.tensor_tensor(tick_p[:, LT * s + k + 1:LT * s + k + 2], tick_p[:, 0:1], tick_p[:, 0:1], ALU.add)
                            tri = probs[k][:, :, 0:P]
                            pool.affine_select(out=tri, in_=tri, compare_op=ALU.is_ge, fill=0.0, base=0,
                                               pattern=[[0, GH], [1, P]], channel_multiplier=-1).then_inc(a_sel, 1)
                        if k == 0 and has(n, 1):
                            if has(n, 3):
                                wait(pool, a_pv, 4 * (at - 2))
                            if s == 0:
                                gather(i - 1, U - 1)
                            else:
                                gather(i, s - 1)

                steps(pool, step)

            @block.tensor
            def _(pe):
                def scores(i, s, u):
                    at = U * i + s
                    r, h0, heads = fills[u]
                    bank = s1[u % BANKS][:, 0:heads * r * P].rearrange("p (h t) -> p h t", h=heads)
                    if u == 0:
                        pe.wait_ge(a_load[s], 96 * (i + 1))
                    wait(pe, a_max, bank_free(at, u))
                    for h in range(heads):
                        pe.matmul(bank[:, h, :], qs[0:ROWS, s, h0 + h, (r - 1) * P:r * P],
                                  ks[0:ROWS, s, h0 + h, 0:r * P], start=True, stop=False, skip_group_check=True)
                    pe.matmul(bank[:, :, (r - 1) * P:r * P], identb[:, :], later_keys[:, 0:heads, :],
                              start=False, stop=True, skip_group_check=True).then_inc(a_s1, 1)

                def shifted(i, s, n, u):
                    at = U * i + s - 2
                    sl = (s - 2) % U
                    r, h0, heads = fills[u]
                    k = LT - r
                    bank = s2[u % BANKS][:, 0:heads * r * P].rearrange("p (h t) -> p h t", h=heads)
                    if u == 0:
                        pe.wait_ge(a_mrow[sl], 32 * (i + 1) if s >= 2 else 32 * i)
                        if n is not None and n < 2 + SLOTS:
                            pe.wait_ge(a_kones, sl + 1)
                    wait(pe, a_exp, bank_free(at, u))
                    for h in range(heads):
                        mm = pe.matmul(bank[:, h, :], ks[0:MROWS, sl, h0 + h, k * P:(k + 1) * P],
                                       qs[0:MROWS, sl, h0 + h, k * P:L], start=True, stop=True)
                    mm.then_inc(a_s2, 1)

                def products(at, par, k):
                    pe.wait_ge(a_sel, 4 * at + k + 1)
                    if k == 0:
                        pe.wait_ge(a_vals, at + 1)
                        wait(pe, a_oev, at)
                    for h in range(GH):
                        mm = pe.matmul(o_ps[2 * HD * h:2 * HD * (h + 1), k * P:L], vals[:, par, k, h, :],
                                       probs[k][:, h, :], start=k == 0, stop=k == LT - 1, skip_group_check=True)
                    mm.then_inc(a_pv, 1)

                def step(i, s, n):
                    at = U * i + s
                    for u in range(F):
                        if has(n, 0):
                            scores(i, s, u)
                        if has(n, 2):
                            shifted(i, s, n, u)
                        if u in (0, 1) and has(n, 3):
                            products(at - 3, (s - 3) % 2, 2 + u)
                        if u == 2 and has(n, 1):
                            pe.wait_ge(a_max, F * at)
                            wait(pe, a_norm, at - 3)
                            pe.transpose(misc[0:GH * LT, 0:P], mx[:, (s - 1) % 2, :], identf[:, :]).then_inc(a_mT, 1)
                        if u == 8 and has(n, 3):
                            pe.wait_ge(a_oev, at - 2)
                            if has(n, 1):
                                pe.wait_ge(a_nml, at)
                            else:
                                pe.wait_ge(a_norm, at - 3)
                            for t in range(LT):
                                mm = pe.transpose(misc[:, t * P:(t + 1) * P], oT[:, (s - 3) % 2, t * P:(t + 1) * P], identf[:, :])
                            mm.then_inc(a_oT, 1)
                        if u in (7, 10) and has(n, 2):
                            products(at - 2, (s - 2) % 2, (u - 7) // 3)

                steps(pe, step)

            @block.scalar
            def _(act):
                def step(i, s, n):
                    at = U * i + s
                    for u in range(F):
                        if has(n, 2):
                            r, h0, heads = fills[u]
                            k = LT - r
                            act.wait_ge(a_s2, F * (at - 2) + u + 1)
                            wait(act, a_pv, 4 * (at - 3) + k + 1)
                            act.activation(probs[k][:, h0:h0 + heads, :],
                                           s2[u % BANKS][:, 0:heads * r * P].rearrange("p (h t) -> p h t", h=heads),
                                           ACT.Exp, scale=float(HD) ** -0.5).then_inc(a_exp, 1)
                        if u == 3 and has(n, 3):
                            act.wait_ge(a_pv, 4 * (at - 2))
                            wait(act, a_oT, at - 4)
                            act.activation(oT[:, (s - 3) % 2, :], o_ps[:, :], ACT.Copy).then_inc(a_oev, 1)
                        if u == 4 and has(n, 1):
                            act.wait_ge(a_mT, at)
                            if n is None or n >= 3:
                                sl = (s - 3) % U
                                act.wait_ge(a_mrow[sl], 32 * (i + 1) if s >= 3 else 32 * i)
                            act.activation(nm[:, (s - 1) % 2, 0, :], misc[0:GH * LT, 0:P], ACT.Copy,
                                           scale=-1.0).then_inc(a_nmh, 1)

                steps(act, step)

            @block.vector
            def _(dve):
                def step(i, s, n):
                    at = U * i + s
                    maxima = mx[:, s % 2, :].rearrange("p (h q) -> p h q", h=GH)
                    for u in range(F):
                        if has(n, 0):
                            r, h0, heads = fills[u]
                            if u == 0:
                                wait(dve, a_mT, at - 1)
                            dve.wait_ge(a_s1, F * at + u + 1)
                            dve.tensor_reduce(maxima[:, h0:h0 + heads, r - 1],
                                              s1[u % BANKS][:, 0:heads * r * P].rearrange("p (h t) -> p h t", h=heads),
                                              AX.X, ALU.max).then_inc(a_max, 1)
                        if u == 5 and has(n, 1):
                            dve.wait_ge(a_nmh, at)
                            dve.scalar_tensor_tensor(out=nm[:, (s - 1) % 2, 1, :], in0=misc[0:GH * LT, 0:P], scalar=-1.0,
                                                     in1=nm[:, (s - 1) % 2, 0, :], op0=ALU.mult, op1=ALU.subtract).then_inc(a_nml, 1)
                        if u == 9 and has(n, 3):
                            dve.wait_ge(a_oT, at - 2)
                            sums = misc[:, :].rearrange("p (t h e) -> p t h e", t=LT, h=GH)
                            r = rden[:, s % 2, :, :]
                            dve.reciprocal(r, sums[:, :, :, HD]).then_inc(a_den, 1)
                            dve.wait_ge(a_den, at - 2)
                            g, gi = ((s - 3) % U, i if s >= 3 else i - 1)
                            dst = attn[:, (g // 2) * LT:(g // 2 + 1) * LT, bass.ds((8 * gi + 4 * (g % 2)) * HD, GH * HD)]
                            dve.tensor_tensor(dst.rearrange("p t (h d) -> p t h d", h=GH), sums[:, :, :, 0:HD],
                                              r.unsqueeze(3).to_broadcast([P, LT, GH, HD]), ALU.mult).then_inc(a_norm, 1)

                steps(dve, step)

        ph = ExitStack()
        with ph:
            STAGES = TT // 2 + 1
            ds_n = sb("ds_n", [P, D], F32, ph)
            attnT = sb("attnT", [P, 2, KT, P], F32, ph)
            y1 = sb("y1", [P, LT, D], F32, ph)
            x2 = sb("x2", [P, 2, D], F32, ph)
            xh = sb("xh", [P, 4, 2, D], F16, ph)
            x2T = sb("x2T", [P, 2, KT, TOK], F16, ph)
            down_t = sb("down_t", [P, HT, D], F32R, ph)
            stats = sb("stats3", [P, STAGES, 4, 6], F32, ph)
            mv = sb("mv3", [P, STAGES, 4, 2], F32, ph)
            rstd = sb("rstd3", [P, STAGES, 4], F32, ph)
            nmr = sb("nmr3", [P, STAGES, 4], F32, ph)
            rtmp = sb("rtmp3", [P, 2, 4], F32, ph)
            statsF = sb("stats4", [P, TT, 6], F32, ph)
            mvF = sb("mv4", [P, TT, 2], F32, ph)
            rstdF = sb("rstd4", [P, TT], F32, ph)
            nmrF = sb("nmr4", [P, TT], F32, ph)
            silu = sb("silu", [P, 2, L], F32, ph)
            hid = sb("hid", [P, 2, L], F32, ph)
            hidH = sb("hidH", [P, 2, L], F32R, ph)
            hidL = sb("hidL", [P, 2, L], F32R, ph)

            c_down = sem("down_widened")
            c_aT = sem("attn_turned")
            c_aTc = sem("attnT_copied")
            c_y = sem("y_ready")
            c_y1 = sem("y1_ready")
            c_r = sem("stage_rstd_ready")
            c_n1 = sem("y_normed")
            c_x1 = sem("x1_ready")
            c_n2 = sem("x1_normed")
            c_hi = sem("x2_high")
            c_lo = sem("x2_low")
            c_xT = sem("x2_turned")
            c_x2T = sem("x2T_copied")
            f_g = sem("gate_ready")
            f_u = sem("up_ready")
            f_silu = sem("silu_done")
            f_h = sem("hidden_ready")
            f_hh = sem("hidden_high")
            f_hl = sem("hidden_low")
            f_d = sem("down_used_hidden")
            f_y = sem("down_done")
            f_ys = sem("down_scaled")
            f_link = sem("dve_link3")
            f_r = sem("final_rstd_ready")
            f_n = sem("final_normed")
            f_o = sem("out_ready")
            f_st = sem("out_stored")

            y_ps = [ps(f"down_ps{i}", [P, D], F32, ph) for i in range(LT)]
            g_ps = [ps(f"gate_ps{i}", [P, L], F32, ph) for i in range(2)]
            u_ps = [ps(f"up_ps{i}", [P, L], F32, ph) for i in range(2)]
            block = ph.enter_context(nc.Block())

            def turned_bank(t):
                bank = u_ps[t % 2] if t < LT else y_ps[t - LT]
                return bank[:, :].bitcast(F16).rearrange("p (a k t) -> p a k t", a=2, k=KT)

            def hidden_steps(eng, step):
                for b in range(B):
                    step(b, b * HT, 0, 0, 0)
                    step(b, b * HT + 1, 1, 1, 1)
                    with eng.Fori(1, HT // 2) as i:
                        for a in range(2):
                            step(b, b * HT + 2 * i + a, 2 * i + a, a, None)
                    step(b, (b + 1) * HT, None, 0, HT)

            @block.tensor
            def _(pe):
                def turn_attn(t):
                    wait(pe, c_aTc, t - 1)
                    for k in range(KT):
                        mm = pe.transpose(g_ps[t % 2][:, k * P:(k + 1) * P], attn[:, t, k * P:(k + 1) * P], identf[:, :])
                    mm.then_inc(c_aT, 1)

                def project(t):
                    pe.wait_ge(c_aTc, t + 1)
                    wait(pe, c_y1, t - LT + 1)
                    for k in range(KT):
                        mm = pe.matmul(y_ps[t % LT][:, :], attnT[:, t % 2, k, :], wo_sb[:, k, :], start=k == 0, stop=k == KT - 1)
                    mm.then_inc(c_y, 1)

                def turn_x2(t):
                    pe.wait_ge(c_lo, t + 1)
                    if t < LT:
                        wait(pe, c_x2T, t - 1)
                    else:
                        pe.wait_ge(c_y1, t + 1)
                    for part in range(2):
                        for k in range(KT):
                            mm = pe.transpose(turned_bank(t)[:, part, k, :], xh[:, t % 4, part, k * P:(k + 1) * P], ident16[:, :])
                    mm.then_inc(c_xT, 1)

                pe.wait_ge(c_wo, 16)
                turn_attn(0)
                turn_attn(1)
                for t in range(TT):
                    if t == TT - 2:
                        turn_x2(0)
                        turn_x2(1)
                    project(t)
                    if t + 2 < TT:
                        turn_attn(t + 2)
                turn_x2(2)
                turn_x2(3)
                pe.wait_ge(c_x2T, LT)

                def down(b, n, ht, a, first, last):
                    pe.wait_ge(f_hl, n + 1)
                    if first:
                        wait(pe, f_ys, LT * b)
                    for t in range(LT):
                        for p, part in enumerate((hidH, hidL)):
                            mm = pe.matmul(y_ps[t][:, :], part[:, a, t * P:(t + 1) * P], down_t[:, ht, :],
                                           start=first and p == 0, stop=last and p == 1)
                        if last:
                            mm.then_inc(f_y, 1)
                    if not last:
                        mm.then_inc(f_d, 1)

                def step(b, n, ht, a, k):
                    if ht is not None:
                        for w, banks, ready, free in ((gate_t, g_ps, f_g, f_silu), (up_t, u_ps, f_u, f_h)):
                            wait(pe, free, n - 1)
                            for kt in range(KT):
                                for part in range(2):
                                    mm = pe.matmul(banks[a][:, :], w[:, kt, bass.ds(ht * P, P)],
                                                   x2T[:, part, kt, b * L:(b + 1) * L],
                                                   start=kt == 0 and part == 0, stop=kt == KT - 1 and part == 1)
                            mm.then_inc(ready, 1)
                    if b == 0 and k == 1:
                        for t in range(LT, TT):
                            turn_x2(t)
                        pe.wait_ge(c_x2T, TT)
                        pe.wait_ge(c_down, HT // 4)
                    if k != 0:
                        down(b, n - 1, HT - 1 if ht is None else ht - 1, 1 - a, k == 1, k == HT)

                hidden_steps(pe, step)

            @block.scalar
            def _(act):
                def copy_attnT(t):
                    act.wait_ge(c_aT, t + 1)
                    wait(act, c_y, t - 1)
                    act.activation(attnT[:, t % 2, :, :], g_ps[t % 2][:, :].rearrange("p (k t) -> p k t", k=KT),
                                   ACT.Copy).then_inc(c_aTc, 1)

                def copy_x2T(t):
                    act.wait_ge(c_xT, t + 1)
                    act.activation(x2T[:, :, :, t * P:(t + 1) * P], turned_bank(t), ACT.Copy).then_inc(c_x2T, 1)

                def norms(p):
                    act.wait_ge(c_r, p + 1)
                    for i, t in enumerate(range(2 * p, min(2 * p + 2, TT))):
                        act.activation(y1[:, t % LT, :], y1[:, t % LT, :], ACT.Identity, bias=nmr[:, p, i:i + 1],
                                       scale=rstd[:, p, i:i + 1]).then_inc(c_n1, 1)
                    for i, t in enumerate(range(max(2 * p - 2, 0), 2 * p)):
                        wait(act, c_lo, t - 1)
                        act.activation(x2[:, t % 2, :], xr[:, t, :], ACT.Identity, bias=nmr[:, p, 2 + i:3 + i],
                                       scale=rstd[:, p, 2 + i:3 + i]).then_inc(c_n2, 1)
                        act.wait_ge(c_n2, t + 1)
                        wait(act, c_xT, t - 3)
                        act.activation(xh[:, t % 4, 0, :], x2[:, t % 2, :], ACT.Copy).then_inc(c_hi, 1)

                for t in range(LT):
                    copy_attnT(t)
                for p in range(STAGES):
                    norms(p)
                    if p < 2:
                        copy_attnT(LT + 2 * p)
                        copy_attnT(LT + 2 * p + 1)
                    if p in (1, 2):
                        copy_x2T(2 * p - 2)
                        copy_x2T(2 * p - 1)

                def step(b, n, ht, a, k):
                    if b == 0 and k == 1:
                        for t in range(LT, TT):
                            copy_x2T(t)
                    if ht is not None:
                        act.wait_ge(f_g, n + 1)
                        wait(act, f_h, n - 1)
                        act.activation(silu[:, a, :], g_ps[a][:, :], ACT.Silu, scale=gs_n[:, bass.ds(ht, 1)]).then_inc(f_silu, 1)
                        act.wait_ge(f_h, n + 1)
                        wait(act, f_d, n - 1 - b)
                        if b and k in (0, 1):
                            act.wait_ge(f_y, LT * b)
                        act.activation(hidH[:, a, :], hid[:, a, :], ACT.Copy).then_inc(f_hh, 1)
                    if b and k == 1:
                        norm(0)

                def norm(b):
                    act.wait_ge(f_r, b + 1)
                    for t in range(LT):
                        act.activation(y1[:, t, :], y1[:, t, :], ACT.Identity, bias=nmrF[:, b * LT + t:b * LT + t + 1],
                                       scale=rstdF[:, b * LT + t:b * LT + t + 1]).then_inc(f_n, 1)

                hidden_steps(act, step)
                norm(1)

            @block.vector
            def _(dve):
                chain = [0]

                def link(ins):
                    chain[0] += 1
                    ins.then_inc(f_link, 1)
                    dve.wait_ge(f_link, chain[0])

                def mark(ins):
                    chain[0] += 1
                    ins.then_inc(f_link, 1)

                def settle():
                    dve.wait_ge(f_link, chain[0])

                def rstd_of(var, mean, r, m, tmp, done):
                    rsqrt_steps(dve, link, var, r, tmp)
                    dve.scalar_tensor_tensor(out=m, in0=mean, scalar=-1.0, in1=r, op0=ALU.mult, op1=ALU.mult).then_inc(done, 1)

                def norms(p):
                    new = range(2 * p, min(2 * p + 2, TT))
                    old = range(max(2 * p - 2, 0), 2 * p)
                    for t in old:
                        dve.wait_ge(c_n1, t + 1)
                        dve.tensor_tensor(xr[:, t, :], xr[:, t, :], y1[:, t % LT, :], ALU.add).then_inc(c_x1, 1)
                    for i, t in enumerate(old):
                        dve.wait_ge(c_x1, t + 1)
                        mark(dve.bn_stats(stats[:, p, 2 + i, :], xr[:, t, :]))
                    for i, t in enumerate(new):
                        dve.wait_ge(c_y, t + 1)
                        wait(dve, c_x1, t - LT + 1)
                        dve.tensor_tensor(y1[:, t % LT, :], y_ps[t % LT][:, :], bo_sb[:, :], ALU.add).then_inc(c_y1, 1)
                        dve.wait_ge(c_y1, t + 1)
                        mark(dve.bn_stats(stats[:, p, i, :], y1[:, t % LT, :]))
                    slots = slice(0 if new else 2, 4 if old else 2)
                    settle()
                    for i in range(slots.start, slots.stop):
                        mark(dve.bn_aggr(mv[:, p, i, :], stats[:, p, i, :]))
                    settle()
                    rstd_of(mv[:, p, slots, 1], mv[:, p, slots, 0], rstd[:, p, slots], nmr[:, p, slots],
                            rtmp[:, :, slots], c_r)

                dve.wait_ge(c_small, 32)
                link(dve.tensor_scalar(ds_n[:, :], ds_sb[:, :], -1.0, None, ALU.mult))
                for h in range(0, HT, 4):
                    dve.tensor_copy(down_t[:, h:h + 4, :], down_t16[:, h:h + 4, :]).then_inc(c_down, 1)
                dve.wait_ge(c_x, 16)
                for p in range(STAGES):
                    norms(p)

                def finish(b):
                    ts = slice(b * LT, (b + 1) * LT)
                    for t in range(LT):
                        dve.wait_ge(f_y, b * LT + t + 1)
                        wait(dve, f_o, (b - 1) * LT + t + 1)
                        dve.tensor_tensor(y1[:, t, :], y_ps[t][:, :], ds_n[:, :], ALU.mult).then_inc(f_ys, 1)
                        dve.wait_ge(f_ys, b * LT + t + 1)
                        mark(dve.bn_stats(statsF[:, b * LT + t, :], y1[:, t, :]))
                    settle()
                    for t in range(LT):
                        mark(dve.bn_aggr(mvF[:, b * LT + t, :], statsF[:, b * LT + t, :]))
                    settle()
                    rstd_of(mvF[:, ts, 1], mvF[:, ts, 0], rstdF[:, ts], nmrF[:, ts], rtmp, f_r)

                def add(b):
                    for t in range(LT):
                        dve.wait_ge(f_n, b * LT + t + 1)
                        dve.tensor_tensor(xr[:, b * LT + t, :], xr[:, b * LT + t, :], y1[:, t, :], ALU.add).then_inc(f_o, 1)

                def step(b, n, ht, a, k):
                    if ht is not None:
                        dve.wait_ge(f_u, n + 1)
                        dve.wait_ge(f_silu, n + 1)
                        wait(dve, f_hl, n - 1)
                        dve.scalar_tensor_tensor(out=hid[:, a, :], in0=u_ps[a][:, :], scalar=us_n[:, bass.ds(ht, 1)],
                                                 in1=silu[:, a, :], op0=ALU.mult, op1=ALU.mult).then_inc(f_h, 1)
                        dve.wait_ge(f_hh, n + 1)
                        dve.tensor_tensor(hidL[:, a, :], hid[:, a, :], hidH[:, a, :].bitcast(F32), ALU.subtract).then_inc(f_hl, 1)
                    if k == HT:
                        finish(b)
                    if b and k == 1:
                        add(0)

                hidden_steps(dve, step)
                add(1)

            @block.gpsimd
            def _(pool):
                for t in range(TT):
                    pool.wait_ge(c_hi, t + 1)
                    wait(pool, c_xT, t - 3)
                    pool.tensor_tensor(xh[:, t % 4, 1, :], x2[:, t % 2, :], xh[:, t % 4, 0, :], ALU.subtract).then_inc(c_lo, 1)

            @block.sync
            def _(sp):
                for t in range(TT):
                    sp.wait_ge(f_o, t + 1)
                    sp.dma_start(out[t * P:(t + 1) * P, :], xr[:, t, :]).then_inc(f_st, 16)
                sp.wait_ge(f_st, 16 * TT)


def kernel(L0_attn_x, L0_attn_Wq, L0_attn_bq, L0_attn_Wk, L0_attn_bk, L0_attn_Wv, L0_attn_bv, L0_attn_Wo, L0_attn_bo,
           L0_ffn_gate_w, L0_ffn_gate_scale, L0_ffn_up_w, L0_ffn_up_scale, L0_ffn_down_w, L0_ffn_down_scale):
    import numpy as np
    import concourse.bacc as bacc
    from concourse.bass_utils import run_bass_kernel_spmd

    D = L0_attn_x.shape[-1]

    def turned(w):
        wt = np.asarray(w).T
        return np.ascontiguousarray(wt.reshape(-1, P, wt.shape[1]).transpose(1, 0, 2))

    def columns(v):
        return np.ascontiguousarray(np.asarray(v).reshape(-1, P).T)

    def spread(v):
        return np.ascontiguousarray(np.broadcast_to(np.asarray(v).reshape(1, -1), (P, v.size)))

    arrays = {
        "x": np.ascontiguousarray(np.asarray(L0_attn_x).reshape(-1, D)),
        "wqT": turned(L0_attn_Wq), "wkT": turned(L0_attn_Wk), "wvT": turned(L0_attn_Wv), "woT": turned(L0_attn_Wo),
        "bq": columns(L0_attn_bq), "bk": columns(L0_attn_bk), "bv": spread(L0_attn_bv), "bo": spread(L0_attn_bo),
        "gateT": turned(L0_ffn_gate_w), "upT": turned(L0_ffn_up_w), "downT": turned(L0_ffn_down_w),
        "gate_s": columns(L0_ffn_gate_scale), "up_s": columns(L0_ffn_up_scale), "down_s": spread(L0_ffn_down_scale),
    }
    nc = bacc.Bacc("TRN2", target_bir_lowering=False, num_devices=1)
    args = [nc.dram_tensor(f"in_{n}", a.shape, mybir.dt.from_np(a.dtype), kind="ExternalInput").ap() for n, a in arrays.items()]
    out = nc.dram_tensor("out_0", arrays["x"].shape, F32, kind="ExternalOutput").ap()
    sandwich_block(nc, *args, out)
    r = run_bass_kernel_spmd(nc, [{f"in_{n}": a for n, a in arrays.items()}], core_ids=[0])
    return r.results[0]["out_0"].reshape(np.asarray(L0_attn_x).shape)
```

```python
from contextlib import ExitStack

import concourse.bass as bass
from concourse import mybir

F32 = mybir.dt.float32
F32R = mybir.dt.float32r
BF16 = mybir.dt.bfloat16
F16 = mybir.dt.float16
I32 = mybir.dt.int32
ALU = mybir.AluOpType
ACT = mybir.ActivationFunctionType
AX = mybir.AxisListType

P = 128
EPS = 1e-5
MASKED = -1e30
RSQRT_MAGIC = float(0x5F3759DF)
THRESH_FACTOR = 0.7

RUNS = ((0, 0, 3), (0, 1, 2), (0, 2, 1))


def wait(eng, sem, value):
    if isinstance(value, int) and value <= 0:
        return
    eng.wait_ge(sem, value)


def sandwich_block(nc, x, wqT, wkT, wvT, woT, bq, bk, bv, bo, gateT, upT, downT, gate_s, up_s, down_s, out):
    TOK, D = x.shape
    B = 2
    L = TOK // B
    H = 32
    HD = D // H
    KT = D // P
    TT = TOK // P
    LT = L // P
    HID = gateT.shape[2]
    HT = HID // P
    GH = 4
    NG = H // GH * B
    ROWS = sum(n for _, _, n in RUNS) * HD
    MROWS = ROWS + 2
    SLOTS = 4

    q_parts = nc.dram_tensor("q_parts", [H, 3 * HD, TOK], BF16, kind="Internal").ap()
    k_parts = nc.dram_tensor("k_parts", [H, 3 * HD, TOK], BF16, kind="Internal").ap()

    ctx = ExitStack()
    with ctx:
        def sb(name, shape, dt, stack=ctx):
            return stack.enter_context(nc.sbuf_tensor(name, shape, dt))

        def ps(name, shape, dt, stack):
            return stack.enter_context(nc.psum_tensor(name, shape, dt))

        def sem(name):
            return ctx.enter_context(nc.semaphore(name))

        identf = sb("identf", [P, P], F32)
        identb = sb("identb", [P, P], BF16)
        later_keys = sb("later_keys", [P, GH, P], BF16)
        v_sb = sb("v_sb", [P, TT, D], F32)
        gate_t = sb("gate_t", [P, KT, HID], F16)
        up_t = sb("up_t", [P, KT, HID], F16)
        down_t16 = sb("down_t16", [P, HT, D], BF16)
        gs_n = sb("gs_n", [P, HT], F32)
        us_n = sb("us_n", [P, HT], F32)
        bv_sb = sb("bv_sb", [P, D], F32)
        w_sb = sb("w_sb", [P, 2, 2, KT, D], F32R)
        operands = w_sb[:, :, :, :, :].bitcast(BF16).rearrange("p a b k d -> p (a b k d)").rearrange(
            "p (s o h t) -> p s o h t", s=SLOTS, o=2, h=GH)

        def qs(s):
            return operands[:, (s + 2) % SLOTS, 0, :, :]

        def ks(s):
            return operands[:, (s + 2) % SLOTS, 1, :, :]

        a_load = [sem(f"parts_loaded{i}") for i in range(SLOTS)]

        def load_operands(sp, i, s):
            h0 = 8 * i + 4 * (s % 2)
            t0 = (s // 2) * L
            row = 0
            for q0, k0, n in RUNS:
                for dst, src, first in ((qs(s), q_parts, q0), (ks(s), k_parts, k0)):
                    rows = src[bass.ds(h0, GH), first * HD:(first + n) * HD, t0:t0 + L]
                    sp.dma_start(dst[row:row + n * HD, :, :], rows.rearrange("h r t -> r h t")).then_inc(a_load[s], 16)
                row += n * HD

        def rsqrt_steps(eng, link, var, y, tmp):
            w = tmp[:, 0, :]
            a = tmp[:, 1, :]
            link(eng.tensor_scalar(w, var, EPS, None, ALU.add))
            link(eng.tensor_scalar(a.bitcast(I32), w.bitcast(I32), 1, None, ALU.logical_shift_right))
            link(eng.tensor_scalar(y.bitcast(I32), a.bitcast(I32), -1.0, RSQRT_MAGIC, ALU.mult, ALU.add))
            for _ in range(3):
                link(eng.tensor_tensor(a, y, w, ALU.mult))
                link(eng.scalar_tensor_tensor(out=a, in0=a, scalar=-0.5, in1=y, op0=ALU.mult, op1=ALU.mult))
                link(eng.scalar_tensor_tensor(out=y, in0=a, scalar=1.5, in1=y, op0=ALU.add, op1=ALU.mult))

        ph = ExitStack()
        with ph:
            xs = v_sb
            xT = sb("xT", [P, 2, KT, TOK], F32R, ph)
            bq_sb = sb("bq_sb", [P, KT], F32, ph)
            bk_sb = sb("bk_sb", [P, KT], F32, ph)
            stats = sb("stats", [P, LT, 6], F32, ph)
            mv = sb("mv", [P, TT, 2], F32, ph)
            rstd = sb("rstd", [P, TT], F32, ph)
            rtmp = sb("rtmp", [P, 2, LT], F32, ph)
            TB = 3
            RB = 3
            rest = sb("rest", [P, RB, L], F32, ph)
            PB = 4
            parts = sb("parts", [P, PB, 3, L], BF16, ph)
            CH = 4
            CW = KT * HID // CH
            RAW = 6
            raw = sb("raw", [P, RAW, CW], F32, ph)
            above = sb("above", [P, CW], BF16, ph)
            junk = sb("junk", [P, CW], BF16, ph)
            asum = sb("asum", [P, 3 * CH], F32, ph)
            ones = sb("ones", [P, P], F32, ph)
            tot = sb("tot", [P, 3], F32, ph)
            thr = sb("thr", [P, 3], F32, ph)
            nthr = sb("nthr", [P, 3], F32, ph)

            turned = [ps(f"turned{i}", [P, L], F32, ph) for i in range(TB)]
            proj = [ps(f"proj{i}", [P, L], F32, ph) for i in range(4)]
            abs_total = ps("abs_total", [P, CH], F32, ph)

            s_x = [sem(f"x_loaded{t}") for t in range(TT)]
            s_small = sem("small_loaded")
            s_raw = [sem(f"raw_loaded{i}") for i in range(RAW + 2)]
            s_ident = sem("ident_made")
            s_ones = sem("ones_made")
            s_mask = sem("mask_made")
            s_link = sem("dve_link")
            s_xn = sem("x_normed")
            s_turn = sem("x_turned")
            s_xH = sem("x_high_copied")
            s_xL = sem("x_low_ready")
            s_wH = sem("w_high_ready")
            s_wL = sem("w_low_ready")
            s_proj = sem("proj_ready")
            s_hi = sem("high_ready")
            s_rest = sem("rest_ready")
            s_mid = sem("mid_ready")
            s_low = sem("low_ready")
            s_vev = sem("v_copied")
            s_parts = [sem(f"parts_stored{i}") for i in range(PB)]
            s_asum = sem("abs_summed")
            s_abst = sem("abs_total_ready")
            s_thr = sem("thr_ready")
            s_above = sem("above_ready")
            s_above_p = sem("above_ready_by_gpsimd")
            s_v = sem("v_bias_added")
            s_tern = sem("ternary_ready")

            units = []
            for kind in "qk":
                units += [(kind, c, b) for b in range(B) for c in range(KT)]
            NQK = len(units)
            units += [("v", t, t // LT) for t in range(TT)]

            buffer_of = {"q": 0, "k": 1, 0: 2, 1: 3, 2: 4, 3: 5, 4: 0, 5: 1, 6: 6, 7: 7, "v": 2, 8: 3, 9: 4, 10: 5, 11: 0}
            items = list(buffer_of)
            raw_src = [gateT, upT, downT.rearrange("p (a h) d -> p a (h d)", a=CH)]
            v_raw = v_sb[:, :, :].rearrange("p (a t) d -> p a (t d)", a=2)

            def raw_buffer(item):
                i = buffer_of[item]
                return raw[:, i, :] if i < RAW else v_raw[:, i - RAW, :]

            def holders(item):
                return [o for o in items[:items.index(item)] if buffer_of[o] == buffer_of[item]]

            def wait_raw(eng, item):
                eng.wait_ge(s_raw[buffer_of[item]], 16 * (len(holders(item)) + 1))

            sums_after = {5: 0, 9: 1, 17: 2}
            act_after = {0: [0], 2: [1, 2], 3: [3], 4: [4], 5: [5], 6: [6], 7: [7], 9: ["v"], 10: [8], 11: [9], 12: [10],
                         13: [11]}
            dve_with = {5: [("t", 0), 0], 6: [1], 8: [2], 9: [3], 10: [("t", 1), 4], 11: [5], 12: [6], 14: [7],
                        17: [("t", 2), 8], 20: [9], 21: [10], 22: [11]}
            pool_with = {9: ["v"], 17: [11]}
            loads_after = {1: [6, 7], 5: ["v"], 6: [8], 7: [9], 8: [10], 9: [11]}

            block = ph.enter_context(nc.Block())

            @block.sync
            def _(sp):
                def load_x(t):
                    sp.dma_start(xs[:, t, :], x[t * P:(t + 1) * P, :]).then_inc(s_x[t], 16)

                def load_raw(item):
                    for before in holders(item)[-1:]:
                        if before in ("q", "k", "v"):
                            sp.wait_ge(s_wL, "qkv".index(before) + 1)
                        else:
                            sp.wait_ge(s_tern, before + 1)
                    if buffer_of[item] >= RAW:
                        sp.wait_ge(s_turn, TT)
                    if item in ("q", "k", "v"):
                        src = (wqT, wkT, wvT)["qkv".index(item)].rearrange("p k d -> p (k d)")
                    else:
                        src = raw_src[item // CH][:, item % CH, :]
                    sp.dma_start(raw_buffer(item), src).then_inc(s_raw[buffer_of[item]], 16)

                for t in range(LT):
                    load_x(t)
                load_raw("q")
                for t in range(LT, TT):
                    load_x(t)
                load_raw("k")
                sp.dma_start(bq_sb[:, :], bq).then_inc(s_small, 16)
                sp.dma_start(bk_sb[:, :], bk).then_inc(s_small, 16)
                sp.dma_start(bv_sb[:, :], bv).then_inc(s_small, 16)
                sp.dma_start(gs_n[:, :], gate_s).then_inc(s_small, 16)
                sp.dma_start(us_n[:, :], up_s).then_inc(s_small, 16)
                for j in range(6):
                    load_raw(j)
                for n, (kind, c, b) in enumerate(units[:NQK]):
                    sp.wait_ge(s_low, n + 1)
                    for part in range(3):
                        row = HD * (part if kind == "q" else 2 - part)
                        dst = (q_parts if kind == "q" else k_parts)[8 * c:8 * c + 8, row:row + HD, b * L:(b + 1) * L]
                        sp.dma_start(dst, parts[:, n % PB, part, :]).then_inc(s_parts[n % PB], 16)
                    for item in loads_after.get(n, []):
                        load_raw(item)
                for i in range(PB):
                    sp.wait_ge(s_parts[i], 48 * len(range(i, NQK, PB)))
                sp.wait_ge(s_proj, NQK)
                load_operands(sp, 0, 0)
                load_operands(sp, 0, 1)

            @block.gpsimd
            def _(pool):
                pool.memset(identf[:, :], 0.0).then_inc(s_ident, 1)
                pool.wait_ge(s_ident, 1)
                pool.affine_select(out=identf[:, :], in_=identf[:, :], compare_op=ALU.not_equal, fill=1.0,
                                   base=0, pattern=[[-1, P]], channel_multiplier=1).then_inc(s_ident, 1)
                pool.wait_ge(s_ident, 2)
                pool.tensor_copy(identb[:, :], identf[:, :]).then_inc(s_ident, 1)
                pool.memset(ones[:, :], 1.0).then_inc(s_ones, 1)

                def w_low(m):
                    pool.wait_ge(s_wH, m + 1)
                    pool.tensor_tensor(w_sb[:, m % 2, 1, :, :], raw_buffer("qkv"[m]).rearrange("p (k d) -> p k d", k=KT),
                                       w_sb[:, m % 2, 0, :, :].bitcast(F32), ALU.subtract).then_inc(s_wL, 1)

                w_low(0)
                w_low(1)
                pool.memset(later_keys[:, :, :], 0.0).then_inc(s_mask, 1)
                pool.wait_ge(s_mask, 1)
                pool.affine_select(out=later_keys[:, :, :], in_=later_keys[:, :, :], compare_op=ALU.is_ge, fill=MASKED,
                                   base=0, pattern=[[0, GH], [-1, P]], channel_multiplier=1).then_inc(s_mask, 1)

                def low_part(n):
                    pool.wait_ge(s_mid, n + 1)
                    pool.tensor_tensor(parts[:, n % PB, 2, :], rest[:, n % RB, :], parts[:, n % PB, 1, :],
                                       ALU.subtract).then_inc(s_low, 1)

                def add_bias(n):
                    t = units[n][1]
                    pool.wait_ge(s_vev, n - NQK + 1)
                    pool.tensor_tensor(v_sb[:, t, :], v_sb[:, t, :], bv_sb[:, :], ALU.add).then_inc(s_v, 1)

                def compare(j):
                    pool.wait_ge(s_thr, j // CH + 1)
                    pool.wait_ge(s_asum, 3 * CH)
                    pool.tensor_scalar(junk[:, :], raw_buffer(j), thr[:, j // CH:j // CH + 1], None, ALU.is_gt).then_inc(s_above_p, 1)

                for n in range(len(units)):
                    if 0 < n <= NQK:
                        low_part(n - 1)
                    if NQK < n <= NQK + LT:
                        add_bias(n - 1)
                    for j in pool_with.get(n, []):
                        if j == "v":
                            w_low(2)
                        else:
                            compare(j)

            @block.tensor
            def _(pe):
                pe.wait_ge(s_ident, 2)
                pe.wait_ge(s_ones, 1)

                def turn(t):
                    pe.wait_ge(s_xn, t + 1)
                    wait(pe, s_xL, t - TB + 1)
                    for k in range(KT):
                        mm = pe.transpose(turned[t % TB][:, k * P:(k + 1) * P], xs[:, t, k * P:(k + 1) * P], identf[:, :])
                    mm.then_inc(s_turn, 1)

                def threshold_sum(m):
                    pe.wait_ge(s_asum, CH * (m + 1))
                    wait(pe, s_thr, m)
                    pe.matmul(abs_total[:, :], ones[:, :], asum[:, CH * m:CH * m + CH], start=True, stop=True).then_inc(s_abst, 1)

                for t in range(LT):
                    turn(t)
                for n, (kind, c, b) in enumerate(units):
                    if n == 3:
                        for t in range(LT, TT):
                            turn(t)
                    m = "qkv".index(kind)
                    pe.wait_ge(s_wL, m + 1)
                    pe.wait_ge(s_xL, LT * (b + 1))
                    wait(pe, s_rest, min(n - 3, NQK))
                    wait(pe, s_vev, n - 3 - NQK)
                    for k in range(KT):
                        for xp, wp in ((0, 0), (0, 1), (1, 0)):
                            first, last = k == 0 and xp + wp == 0, k == KT - 1 and xp == 1
                            if kind == "v":
                                mm = pe.matmul(proj[n % 4][:, :], xT[:, xp, k, c * P:(c + 1) * P], w_sb[:, m % 2, wp, k, :],
                                               start=first, stop=last)
                            else:
                                mm = pe.matmul(proj[n % 4][:, :], w_sb[:, m % 2, wp, k, c * P:(c + 1) * P],
                                               xT[:, xp, k, b * L:(b + 1) * L], start=first, stop=last)
                    mm.then_inc(s_proj, 1)
                    if n in sums_after:
                        threshold_sum(sums_after[n])

            @block.scalar
            def _(act):
                def w_high(m):
                    wait_raw(act, "qkv"[m])
                    if m == 2:
                        act.wait_ge(s_proj, KT * B)
                    act.activation(w_sb[:, m % 2, 0, :, :], raw_buffer("qkv"[m]).rearrange("p (k d) -> p k d", k=KT),
                                   ACT.Copy).then_inc(s_wH, 1)

                def x_high(t):
                    act.wait_ge(s_turn, t + 1)
                    act.activation(xT[:, 0, :, t * P:(t + 1) * P],
                                   turned[t % TB][:, :].rearrange("p (k t) -> p k t", k=KT), ACT.Copy).then_inc(s_xH, 1)

                def abs_sum(j):
                    wait_raw(act, j)
                    if j:
                        act.wait_ge(s_asum, j)
                    act.activation(junk[:, :], raw_buffer(j), ACT.Abs, accum_out=asum[:, j:j + 1]).then_inc(s_asum, 1)

                def high_part(n, kind, c):
                    act.wait_ge(s_proj, n + 1)
                    wait(act, s_parts[n % PB], 48 * (n // PB))
                    bias = bq_sb if kind == "q" else bk_sb
                    act.activation(parts[:, n % PB, 0, :], proj[n % 4][:, :], ACT.Identity,
                                   bias=bias[:, c:c + 1]).then_inc(s_hi, 1)

                def mid_part(n):
                    act.wait_ge(s_rest, n + 1)
                    act.activation(parts[:, n % PB, 1, :], rest[:, n % RB, :], ACT.Copy).then_inc(s_mid, 1)

                w_high(0)
                for t in range(LT):
                    x_high(t)
                w_high(1)
                act.wait_ge(s_small, 80)
                for n, (kind, c, b) in enumerate(units):
                    if n == 2:
                        for t in range(LT, TT):
                            x_high(t)
                    if n < NQK:
                        high_part(n, kind, c)
                    else:
                        if n == NQK:
                            act.wait_ge(s_tern, 8)
                        act.wait_ge(s_proj, n + 1)
                        act.activation(v_sb[:, c, :], proj[n % 4][:, :], ACT.Copy).then_inc(s_vev, 1)
                    if 0 < n <= NQK:
                        mid_part(n - 1)
                    for j in act_after.get(n, []):
                        if j == "v":
                            w_high(2)
                        else:
                            abs_sum(j)

            @block.vector
            def _(dve):
                chain = [0]

                def link(ins):
                    chain[0] += 1
                    ins.then_inc(s_link, 1)
                    dve.wait_ge(s_link, chain[0])

                def norm(b):
                    for t in range(b * LT, (b + 1) * LT):
                        dve.wait_ge(s_x[t], 16)
                        link(dve.bn_stats(stats[:, t % LT, :], xs[:, t, :]))
                        link(dve.bn_aggr(mv[:, t, :], stats[:, t % LT, :]))
                    rsqrt_steps(dve, link, mv[:, b * LT:(b + 1) * LT, 1], rstd[:, b * LT:(b + 1) * LT], rtmp)
                    for t in range(b * LT, (b + 1) * LT):
                        dve.tensor_scalar(xs[:, t, :], xs[:, t, :], mv[:, t, 0:1], rstd[:, t:t + 1],
                                          ALU.subtract, ALU.mult).then_inc(s_xn, 1)

                def x_low(t):
                    dve.wait_ge(s_xH, t + 1)
                    dve.tensor_tensor(xT[:, 1, :, t * P:(t + 1) * P], turned[t % TB][:, :].rearrange("p (k t) -> p k t", k=KT),
                                      xT[:, 0, :, t * P:(t + 1) * P].bitcast(F32), ALU.subtract).then_inc(s_xL, 1)

                def threshold(m):
                    dve.wait_ge(s_abst, m + 1)
                    link(dve.tensor_reduce(tot[:, m:m + 1], abs_total[:, :], AX.X, ALU.add))
                    link(dve.tensor_scalar(thr[:, m:m + 1], tot[:, m:m + 1], 1.0 / (P * KT * HID), THRESH_FACTOR,
                                           ALU.mult, ALU.mult))
                    dve.tensor_scalar(nthr[:, m:m + 1], thr[:, m:m + 1], -1.0, None, ALU.mult).then_inc(s_thr, 1)
                    dve.wait_ge(s_thr, m + 1)

                down_v = down_t16[:, :, :].rearrange("p (a h) d -> p a (h d)", a=CH)
                dests = [gate_t, up_t, down_v]

                def ternary(j):
                    m = j // CH
                    if j == 11:
                        over = junk
                        dve.wait_ge(s_above_p, 1)
                    else:
                        over = above
                        wait(dve, s_tern, j)
                        dve.tensor_scalar(above[:, :], raw_buffer(j), thr[:, m:m + 1], None, ALU.is_gt).then_inc(s_above, 1)
                        dve.wait_ge(s_above, j + 1)
                    dve.scalar_tensor_tensor(out=dests[m][:, j % CH, :], in0=raw_buffer(j), scalar=nthr[:, m:m + 1],
                                             in1=over[:, :], op0=ALU.is_lt, op1=ALU.subtract).then_inc(s_tern, 1)

                def rest_part(n, kind, c):
                    dve.wait_ge(s_hi, n + 1)
                    wait(dve, s_low, n - RB + 1)
                    bias = bq_sb if kind == "q" else bk_sb
                    dve.scalar_tensor_tensor(out=rest[:, n % RB, :], in0=proj[n % 4][:, :], scalar=bias[:, c:c + 1],
                                             in1=parts[:, n % PB, 0, :], op0=ALU.add, op1=ALU.subtract).then_inc(s_rest, 1)

                norm(0)
                for t in range(LT):
                    x_low(t)
                norm(1)
                dve.wait_ge(s_small, 80)
                dve.tensor_scalar(gs_n[:, :], gs_n[:, :], -1.0, None, ALU.mult)
                dve.tensor_scalar(us_n[:, :], us_n[:, :], -1.0, None, ALU.mult)
                for n, (kind, c, b) in enumerate(units):
                    if n == 2:
                        for t in range(LT, TT):
                            x_low(t)
                    if kind != "v":
                        rest_part(n, kind, c)
                    for w in dve_with.get(n, []):
                        if isinstance(w, tuple):
                            threshold(w[1])
                        else:
                            ternary(w)

        attn = sb("attn", [P, TT, D], F32)
        wo_sb = sb("wo_sb", [P, KT, D], F32)
        bo_sb = sb("bo_sb", [P, D], F32)
        ds_sb = sb("ds_sb", [P, D], F32)
        xr = sb("xr", [P, TT, D], F32)
        c_wo = sem("wo_loaded")
        c_small = sem("small3_loaded")
        c_x = sem("x_reloaded")
        ph = ExitStack()
        with ph:
            tick_p = sb("tick_p", [P, 1 + LT * SLOTS], F32, ph)
            mx = sb("mx", [P, 2, GH * LT], F32, ph)
            nm = sb("nm", [GH * LT, 2, 2, P], BF16, ph)
            probs = [sb(f"probs{k}", [P, GH, L - k * P], F32, ph) for k in range(LT)]
            vals = sb("vals", [P, 2, LT, GH, 2 * HD], F32, ph)
            oT = sb("oT", [P, 2, L], F32, ph)
            rden = sb("rden", [P, 2, LT, GH], F32, ph)

            s1 = [ps(f"s1_{i}", [P, L], F32, ph) for i in range(3)]
            s2 = [ps(f"s2_{i}", [P, L], F32, ph) for i in range(3)]
            o_ps = ps("o_ps", [P, L], F32, ph)
            misc = ps("misc", [P, L], F32, ph)

            a_mrow = [sem(f"max_rows_placed{i}") for i in range(SLOTS)]
            a_kones = sem("key_ones_made")
            a_v = sem("v_bias_added2")
            a_vones = sem("value_ones_made")
            a_s1 = sem("scores_ready")
            a_max = sem("max_done")
            a_mT = sem("max_turned")
            a_nmh = sem("neg_max_high")
            a_nml = sem("neg_max_mid")
            a_s2 = sem("shifted_scores_ready")
            a_exp = sem("exp_done")
            a_sel = sem("later_keys_cleared")
            a_vals = sem("values_gathered")
            a_pv = sem("pv_done")
            a_oev = sem("sums_copied")
            a_oT = sem("sums_turned")
            a_den = sem("denominators_inverted")
            a_norm = sem("group_normalised")

            fills = []
            for r in range(LT, 0, -1):
                heads = 1 << ((LT // r).bit_length() - 1)
                fills += [(r, h, heads) for h in range(0, GH, heads)]
            F = len(fills)
            BANKS = 3
            done_fills = [sum(f[0] >= LT - k for f in fills) for k in range(LT)]

            def bank_free(at, u):
                last = max((v for v in range(F) if v % BANKS == u % BANKS), default=0)
                return F * at + u - BANKS + 1 if u >= BANKS else F * (at - 1) + last + 1

            U = SLOTS

            def steps(eng, step):
                for s in range(U):
                    step(0, s, s)
                with eng.Fori(1, NG // U) as i:
                    for s in range(U):
                        step(i, s, None)
                for s in range(3):
                    step(NG // U, s, NG + s)

            def has(n, lag):
                return n is None or 0 <= n - lag < NG

            block = ph.enter_context(nc.Block())

            @block.sync
            def _(sp):
                def step(i, s, n):
                    if has(n, 0) and n not in (0, 1):
                        wait(sp, a_s2, F * (U * i + s - 3))
                        load_operands(sp, i, s)
                    if has(n, 2):
                        m = (s - 2) % U
                        sp.wait_ge(a_nml, U * i + s - 1)
                        for part in range(2):
                            row = qs(m)[ROWS + part:ROWS + part + 1, :, :].rearrange("o h (q t) -> o (h q) t", t=P)
                            sp.dma_start(row, nm[:, s % 2, part, :]).then_inc(a_mrow[m], 16)
                    if n == NG + 1:
                        sp.dma_start(wo_sb[:, :, :], woT).then_inc(c_wo, 16)
                        sp.dma_start(bo_sb[:, :], bo).then_inc(c_small, 16)
                        sp.dma_start(ds_sb[:, :], down_s).then_inc(c_small, 16)
                        sp.dma_start(xr[:, :, :], x.rearrange("(t p) d -> p t d", p=P)).then_inc(c_x, 16)

                steps(sp, step)

            @block.gpsimd
            def _(pool):
                pool.memset(vals[:, :, :, :, :], 1.0).then_inc(a_vones, 1)
                pool.wait_ge(a_vones, 1)
                pool.memset(tick_p[:, :], 0.0).then_inc(a_vones, 1)
                pool.wait_ge(a_vones, 2)
                for s in range(SLOTS):
                    pool.memset(ks(s)[ROWS:P, :, :], 1.0).then_inc(a_kones, 1)
                    pool.wait_ge(a_kones, s + 1)
                for t in range(LT, TT):
                    pool.tensor_tensor(v_sb[:, t, :], v_sb[:, t, :], bv_sb[:, :], ALU.add).then_inc(a_v, 1)
                    pool.wait_ge(a_v, t - LT + 1)

                def gather(i, s):
                    h0 = 8 * i + 4 * (s % 2)
                    t0 = (s // 2) * LT
                    pool.tensor_copy(vals[:, s % 2, :, :, 0:HD],
                                     v_sb[:, t0:t0 + LT, bass.ds(h0 * HD, GH * HD)].rearrange("p t (h d) -> p t h d", h=GH)
                                     ).then_inc(a_vals, 1)

                def step(i, s, n):
                    at = U * i + s
                    for k in range(LT):
                        if has(n, 2):
                            wait(pool, a_exp, F * (at - 2) + done_fills[k])
                            if n is None:
                                pool.tensor_tensor(tick_p[:, LT * s + k + 1:LT * s + k + 2], tick_p[:, 0:1], tick_p[:, 0:1], ALU.add)
                            tri = probs[k][:, :, 0:P]
                            pool.affine_select(out=tri, in_=tri, compare_op=ALU.is_ge, fill=0.0, base=0,
                                               pattern=[[0, GH], [1, P]], channel_multiplier=-1).then_inc(a_sel, 1)
                        if k == 0 and has(n, 1):
                            if has(n, 3):
                                wait(pool, a_pv, 4 * (at - 2))
                            if s == 0:
                                gather(i - 1, U - 1)
                            else:
                                gather(i, s - 1)

                steps(pool, step)

            @block.tensor
            def _(pe):
                def scores(i, s, u):
                    at = U * i + s
                    r, h0, heads = fills[u]
                    bank = s1[u % BANKS][:, 0:heads * r * P].rearrange("p (h t) -> p h t", h=heads)
                    if u == 0:
                        pe.wait_ge(a_load[s], 96 * (i + 1))
                    wait(pe, a_max, bank_free(at, u))
                    for h in range(heads):
                        pe.matmul(bank[:, h, :], qs(s)[0:ROWS, h0 + h, (r - 1) * P:r * P],
                                  ks(s)[0:ROWS, h0 + h, 0:r * P], start=True, stop=False, skip_group_check=True)
                    pe.matmul(bank[:, :, (r - 1) * P:r * P], identb[:, :], later_keys[:, 0:heads, :],
                              start=False, stop=True, skip_group_check=True).then_inc(a_s1, 1)

                def shifted(i, s, n, u):
                    at = U * i + s - 2
                    sl = (s - 2) % U
                    r, h0, heads = fills[u]
                    k = LT - r
                    bank = s2[u % BANKS][:, 0:heads * r * P].rearrange("p (h t) -> p h t", h=heads)
                    if u == 0:
                        pe.wait_ge(a_mrow[sl], 32 * (i + 1) if s >= 2 else 32 * i)
                        if n is not None and n < 2 + SLOTS:
                            pe.wait_ge(a_kones, sl + 1)
                    wait(pe, a_exp, bank_free(at, u))
                    for h in range(heads):
                        mm = pe.matmul(bank[:, h, :], ks(sl)[0:MROWS, h0 + h, k * P:(k + 1) * P],
                                       qs(sl)[0:MROWS, h0 + h, k * P:L], start=True, stop=True)
                    mm.then_inc(a_s2, 1)

                def products(at, par, k):
                    pe.wait_ge(a_sel, 4 * at + k + 1)
                    if k == 0:
                        pe.wait_ge(a_vals, at + 1)
                        wait(pe, a_oev, at)
                    for h in range(GH):
                        mm = pe.matmul(o_ps[2 * HD * h:2 * HD * (h + 1), k * P:L], vals[:, par, k, h, :],
                                       probs[k][:, h, :], start=k == 0, stop=k == LT - 1, skip_group_check=True)
                    mm.then_inc(a_pv, 1)

                def step(i, s, n):
                    at = U * i + s
                    for u in range(F):
                        if has(n, 0):
                            scores(i, s, u)
                        if has(n, 2):
                            shifted(i, s, n, u)
                        if u in (0, 1) and has(n, 3):
                            products(at - 3, (s - 3) % 2, 2 + u)
                        if u == 2 and has(n, 1):
                            pe.wait_ge(a_max, F * at)
                            wait(pe, a_norm, at - 3)
                            pe.transpose(misc[0:GH * LT, 0:P], mx[:, (s - 1) % 2, :], identf[:, :]).then_inc(a_mT, 1)
                        if u == 8 and has(n, 3):
                            pe.wait_ge(a_oev, at - 2)
                            if has(n, 1):
                                pe.wait_ge(a_nml, at)
                            else:
                                pe.wait_ge(a_norm, at - 3)
                            for t in range(LT):
                                mm = pe.transpose(misc[:, t * P:(t + 1) * P], oT[:, (s - 3) % 2, t * P:(t + 1) * P], identf[:, :])
                            mm.then_inc(a_oT, 1)
                        if u in (7, 10) and has(n, 2):
                            products(at - 2, (s - 2) % 2, (u - 7) // 3)

                steps(pe, step)

            @block.scalar
            def _(act):
                def step(i, s, n):
                    at = U * i + s
                    for u in range(F):
                        if has(n, 2):
                            r, h0, heads = fills[u]
                            k = LT - r
                            act.wait_ge(a_s2, F * (at - 2) + u + 1)
                            wait(act, a_pv, 4 * (at - 3) + k + 1)
                            act.activation(probs[k][:, h0:h0 + heads, :],
                                           s2[u % BANKS][:, 0:heads * r * P].rearrange("p (h t) -> p h t", h=heads),
                                           ACT.Exp, scale=float(HD) ** -0.5).then_inc(a_exp, 1)
                        if u == 3 and has(n, 3):
                            act.wait_ge(a_pv, 4 * (at - 2))
                            wait(act, a_oT, at - 4)
                            act.activation(oT[:, (s - 3) % 2, :], o_ps[:, :], ACT.Copy).then_inc(a_oev, 1)
                        if u == 4 and has(n, 1):
                            act.wait_ge(a_mT, at)
                            if n is None or n >= 3:
                                sl = (s - 3) % U
                                act.wait_ge(a_mrow[sl], 32 * (i + 1) if s >= 3 else 32 * i)
                            act.activation(nm[:, (s - 1) % 2, 0, :], misc[0:GH * LT, 0:P], ACT.Copy,
                                           scale=-1.0).then_inc(a_nmh, 1)

                steps(act, step)

            @block.vector
            def _(dve):
                def step(i, s, n):
                    at = U * i + s
                    maxima = mx[:, s % 2, :].rearrange("p (h q) -> p h q", h=GH)
                    for u in range(F):
                        if has(n, 0):
                            r, h0, heads = fills[u]
                            if u == 0:
                                wait(dve, a_mT, at - 1)
                            dve.wait_ge(a_s1, F * at + u + 1)
                            dve.tensor_reduce(maxima[:, h0:h0 + heads, r - 1],
                                              s1[u % BANKS][:, 0:heads * r * P].rearrange("p (h t) -> p h t", h=heads),
                                              AX.X, ALU.max).then_inc(a_max, 1)
                        if u == 5 and has(n, 1):
                            dve.wait_ge(a_nmh, at)
                            dve.scalar_tensor_tensor(out=nm[:, (s - 1) % 2, 1, :], in0=misc[0:GH * LT, 0:P], scalar=-1.0,
                                                     in1=nm[:, (s - 1) % 2, 0, :], op0=ALU.mult, op1=ALU.subtract).then_inc(a_nml, 1)
                        if u == 9 and has(n, 3):
                            dve.wait_ge(a_oT, at - 2)
                            sums = misc[:, :].rearrange("p (t h e) -> p t h e", t=LT, h=GH)
                            r = rden[:, s % 2, :, :]
                            dve.reciprocal(r, sums[:, :, :, HD]).then_inc(a_den, 1)
                            dve.wait_ge(a_den, at - 2)
                            g, gi = ((s - 3) % U, i if s >= 3 else i - 1)
                            dst = attn[:, (g // 2) * LT:(g // 2 + 1) * LT, bass.ds((8 * gi + 4 * (g % 2)) * HD, GH * HD)]
                            dve.tensor_tensor(dst.rearrange("p t (h d) -> p t h d", h=GH), sums[:, :, :, 0:HD],
                                              r.unsqueeze(3).to_broadcast([P, LT, GH, HD]), ALU.mult).then_inc(a_norm, 1)

                steps(dve, step)

        ph = ExitStack()
        with ph:
            STAGES = TT // 2 + 1
            ds_n = sb("ds_n", [P, D], F32, ph)
            ident16 = sb("ident16", [P, P], F16, ph)
            attnT = sb("attnT", [P, 2, KT, P], F32, ph)
            y1 = sb("y1", [P, LT, D], F32, ph)
            x2 = sb("x2", [P, 2, D], F32, ph)
            xh = sb("xh", [P, 4, 2, D], F16, ph)
            x2T = sb("x2T", [P, 2, KT, TOK], F16, ph)
            down_t = w_sb[:, :, :, :, :].rearrange("p a b k d -> p (a b k) d")
            stats = sb("stats3", [P, STAGES, 4, 6], F32, ph)
            mv = sb("mv3", [P, STAGES, 4, 2], F32, ph)
            rstd = sb("rstd3", [P, STAGES, 4], F32, ph)
            nmr = sb("nmr3", [P, STAGES, 4], F32, ph)
            rtmp = sb("rtmp3", [P, 2, 4], F32, ph)
            statsF = sb("stats4", [P, TT, 6], F32, ph)
            mvF = sb("mv4", [P, TT, 2], F32, ph)
            rstdF = sb("rstd4", [P, TT], F32, ph)
            nmrF = sb("nmr4", [P, TT], F32, ph)
            silu = sb("silu", [P, 2, L], F32, ph)
            hid = sb("hid", [P, 2, L], F32, ph)
            hidH = sb("hidH", [P, 2, L], F32R, ph)
            hidL = sb("hidL", [P, 2, L], F32R, ph)

            c_down = sem("down_widened")
            c_ident = sem("ident16_made")
            c_aT = sem("attn_turned")
            c_aTc = sem("attnT_copied")
            c_y = sem("y_ready")
            c_y1 = sem("y1_ready")
            c_r = sem("stage_rstd_ready")
            c_n1 = sem("y_normed")
            c_x1 = sem("x1_ready")
            c_n2 = sem("x1_normed")
            c_hi = sem("x2_high")
            c_lo = sem("x2_low")
            c_xT = sem("x2_turned")
            c_x2T = sem("x2T_copied")
            c_x2T_dve = sem("x2T_copied_by_dve")
            f_g = sem("gate_ready")
            f_u = sem("up_ready")
            f_silu = sem("silu_done")
            f_h = sem("hidden_ready")
            f_hh = sem("hidden_high")
            f_hl = sem("hidden_low")
            f_d = sem("down_used_hidden")
            f_y = sem("down_done")
            f_ys = sem("down_scaled")
            f_link = sem("dve_link3")
            f_r = sem("final_rstd_ready")
            f_n = sem("final_normed")
            f_o = sem("out_ready")
            f_st = sem("out_stored")

            y_ps = [ps(f"down_ps{i}", [P, D], F32, ph) for i in range(LT)]
            g_ps = [ps(f"gate_ps{i}", [P, L], F32, ph) for i in range(2)]
            u_ps = [ps(f"up_ps{i}", [P, L], F32, ph) for i in range(2)]
            block = ph.enter_context(nc.Block())

            def turned_bank(t):
                bank = (u_ps[0], u_ps[1], g_ps[0], g_ps[1], g_ps[0], u_ps[0], g_ps[1], u_ps[1])[t]
                return bank[:, :].bitcast(F16).rearrange("p (a k t) -> p a k t", a=2, k=KT)

            def hidden_steps(eng, step):
                for b in range(B):
                    step(b, b * HT, 0, 0, 0)
                    step(b, b * HT + 1, 1, 1, 1)
                    with eng.Fori(1, HT // 2) as i:
                        for a in range(2):
                            step(b, b * HT + 2 * i + a, 2 * i + a, a, None)
                    step(b, (b + 1) * HT, None, 0, HT)

            @block.tensor
            def _(pe):
                def turn_attn(t):
                    wait(pe, c_aTc, t - 1)
                    for k in range(KT):
                        mm = pe.transpose(g_ps[t % 2][:, k * P:(k + 1) * P], attn[:, t, k * P:(k + 1) * P], identf[:, :])
                    mm.then_inc(c_aT, 1)

                def project(t):
                    pe.wait_ge(c_aTc, t + 1)
                    wait(pe, c_y1, t - LT + 1)
                    for k in range(KT):
                        mm = pe.matmul(y_ps[t % LT][:, :], attnT[:, t % 2, k, :], wo_sb[:, k, :], start=k == 0, stop=k == KT - 1)
                    mm.then_inc(c_y, 1)

                def turn_x2(t):
                    pe.wait_ge(c_lo, t + 1)
                    if 2 <= t < LT:
                        pe.wait_ge(c_aTc, TT)
                    if t >= LT:
                        pe.wait_ge(f_h, HT - 1 + (t - LT) // 2)
                    for part in range(2):
                        for k in range(KT):
                            mm = pe.transpose(turned_bank(t)[:, part, k, :], xh[:, t % 4, part, k * P:(k + 1) * P], ident16[:, :])
                    mm.then_inc(c_xT, 1)

                pe.wait_ge(c_wo, 16)
                pe.wait_ge(c_ident, 1)
                turn_attn(0)
                turn_attn(1)
                for t in range(TT):
                    project(t)
                    if t + 2 < TT:
                        turn_attn(t + 2)
                    if t == TT - 2:
                        turn_x2(0)
                for t in range(1, LT):
                    turn_x2(t)
                pe.wait_ge(c_x2T, LT - 1)
                pe.wait_ge(c_x2T_dve, 1)

                def down(b, n, ht, a, first, last):
                    pe.wait_ge(f_hl, n + 1)
                    if first:
                        wait(pe, f_ys, LT * b)
                    for t in range(LT):
                        for p, part in enumerate((hidH, hidL)):
                            mm = pe.matmul(y_ps[t][:, :], part[:, a, t * P:(t + 1) * P], down_t[:, ht, :],
                                           start=first and p == 0, stop=last and p == 1)
                        if last:
                            mm.then_inc(f_y, 1)
                    if not last:
                        mm.then_inc(f_d, 1)

                def step(b, n, ht, a, k):
                    if b == 1 and k == 0:
                        pe.wait_ge(c_x2T, LT + 1)
                        pe.wait_ge(c_x2T_dve, 3)
                    if ht is not None:
                        for w, banks, ready, free in ((gate_t, g_ps, f_g, f_silu), (up_t, u_ps, f_u, f_h)):
                            wait(pe, free, n - 1)
                            for kt in range(KT):
                                for part in range(2):
                                    mm = pe.matmul(banks[a][:, :], w[:, kt, bass.ds(ht * P, P)],
                                                   x2T[:, part, kt, b * L:(b + 1) * L],
                                                   start=kt == 0 and part == 0, stop=kt == KT - 1 and part == 1)
                            mm.then_inc(ready, 1)
                    if b == 0 and k == 1:
                        pe.wait_ge(c_y1, TT)
                        pe.wait_ge(c_down, HT // 4)
                    if b == 0 and k == HT:
                        turn_x2(LT)
                        turn_x2(LT + 1)
                    if k != 0:
                        down(b, n - 1, HT - 1 if ht is None else ht - 1, 1 - a, k == 1, k == HT)
                    if b == 0 and k == HT:
                        turn_x2(LT + 2)
                        turn_x2(LT + 3)

                hidden_steps(pe, step)

            @block.scalar
            def _(act):
                def copy_attnT(t):
                    act.wait_ge(c_aT, t + 1)
                    wait(act, c_y, t - 1)
                    act.activation(attnT[:, t % 2, :, :], g_ps[t % 2][:, :].rearrange("p (k t) -> p k t", k=KT),
                                   ACT.Copy).then_inc(c_aTc, 1)

                def copy_x2T(t):
                    act.wait_ge(c_xT, t + 1)
                    act.activation(x2T[:, :, :, t * P:(t + 1) * P], turned_bank(t), ACT.Copy).then_inc(c_x2T, 1)

                def norm_y(p):
                    act.wait_ge(c_r, p + 1)
                    for i, t in enumerate(range(2 * p, 2 * p + 2)):
                        act.activation(y1[:, t % LT, :], y1[:, t % LT, :], ACT.Identity, bias=nmr[:, p, i:i + 1],
                                       scale=rstd[:, p, i:i + 1]).then_inc(c_n1, 1)

                def norm_x(p):
                    act.wait_ge(c_r, p + 1)
                    for i, t in enumerate(range(max(2 * p - 2, 0), 2 * p)):
                        wait(act, c_lo, t - 1)
                        act.activation(x2[:, t % 2, :], xr[:, t, :], ACT.Identity, bias=nmr[:, p, 2 + i:3 + i],
                                       scale=rstd[:, p, 2 + i:3 + i]).then_inc(c_n2, 1)
                        act.wait_ge(c_n2, t + 1)
                        wait(act, c_xT, t - 3)
                        act.activation(xh[:, t % 4, 0, :], x2[:, t % 2, :], ACT.Copy).then_inc(c_hi, 1)

                for t in range(LT):
                    copy_attnT(t)
                norm_y(0)
                copy_attnT(LT)
                copy_attnT(LT + 1)
                copy_attnT(LT + 2)
                norm_y(1)
                copy_attnT(LT + 3)
                norm_x(1)
                copy_x2T(0)
                norm_x(2)
                norm_y(2)
                copy_x2T(2)
                copy_x2T(3)

                def step(b, n, ht, a, k):
                    if b == 0 and k == HT:
                        norm_x(STAGES - 1)
                        copy_x2T(LT)
                        copy_x2T(LT + 2)
                    if ht is not None:
                        act.wait_ge(f_g, n + 1)
                        wait(act, f_h, n - 1)
                        act.activation(silu[:, a, :], g_ps[a][:, :], ACT.Silu, scale=gs_n[:, bass.ds(ht, 1)]).then_inc(f_silu, 1)
                        act.wait_ge(f_h, n + 1)
                        wait(act, f_d, n - 1 - b)
                        if b and k in (0, 1):
                            act.wait_ge(f_y, LT * b)
                        act.activation(hidH[:, a, :], hid[:, a, :], ACT.Copy).then_inc(f_hh, 1)
                    if b == 0 and k == 1:
                        norm_y(STAGES - 2)
                        norm_x(STAGES - 2)
                    if b and k == 1:
                        norm(0)

                def norm(b):
                    act.wait_ge(f_r, b + 1)
                    for t in range(LT):
                        act.activation(y1[:, t, :], y1[:, t, :], ACT.Identity, bias=nmrF[:, b * LT + t:b * LT + t + 1],
                                       scale=rstdF[:, b * LT + t:b * LT + t + 1]).then_inc(f_n, 1)

                hidden_steps(act, step)
                norm(1)

            @block.vector
            def _(dve):
                chain = [0]

                def link(ins):
                    chain[0] += 1
                    ins.then_inc(f_link, 1)
                    dve.wait_ge(f_link, chain[0])

                def mark(ins):
                    chain[0] += 1
                    ins.then_inc(f_link, 1)

                def settle():
                    dve.wait_ge(f_link, chain[0])

                def rstd_of(var, mean, r, m, tmp, done):
                    rsqrt_steps(dve, link, var, r, tmp)
                    dve.scalar_tensor_tensor(out=m, in0=mean, scalar=-1.0, in1=r, op0=ALU.mult, op1=ALU.mult).then_inc(done, 1)

                def copy_x2T(t):
                    dve.wait_ge(c_xT, t + 1)
                    dve.tensor_copy(x2T[:, :, :, t * P:(t + 1) * P], turned_bank(t)).then_inc(c_x2T_dve, 1)

                def norms(p):
                    new = range(2 * p, min(2 * p + 2, TT))
                    old = range(max(2 * p - 2, 0), 2 * p)
                    for i, t in enumerate(new):
                        dve.wait_ge(c_y, t + 1)
                        wait(dve, c_x1, t - LT + 1)
                        dve.tensor_tensor(y1[:, t % LT, :], y_ps[t % LT][:, :], bo_sb[:, :], ALU.add).then_inc(c_y1, 1)
                    for i, t in enumerate(new):
                        dve.wait_ge(c_y1, t + 1)
                        mark(dve.bn_stats(stats[:, p, i, :], y1[:, t % LT, :]))
                    if p == 3:
                        copy_x2T(1)
                    for t in old:
                        dve.wait_ge(c_n1, t + 1)
                        dve.tensor_tensor(xr[:, t, :], xr[:, t, :], y1[:, t % LT, :], ALU.add).then_inc(c_x1, 1)
                    for i, t in enumerate(old):
                        dve.wait_ge(c_x1, t + 1)
                        mark(dve.bn_stats(stats[:, p, 2 + i, :], xr[:, t, :]))
                    slots = slice(0 if new else 2, 4 if old else 2)
                    settle()
                    for i in range(slots.start, slots.stop):
                        mark(dve.bn_aggr(mv[:, p, i, :], stats[:, p, i, :]))
                    settle()
                    rsqrt_steps(dve, link, mv[:, p, slots, 1], rstd[:, p, slots], rtmp[:, :, slots])
                    dve.scalar_tensor_tensor(out=nmr[:, p, slots], in0=mv[:, p, slots, 0], scalar=-1.0, in1=rstd[:, p, slots],
                                             op0=ALU.mult, op1=ALU.mult).then_inc(c_r, 1)

                dve.wait_ge(c_small, 32)
                link(dve.tensor_scalar(ds_n[:, :], ds_sb[:, :], -1.0, None, ALU.mult))
                for h in range(0, HT, 4):
                    dve.tensor_copy(down_t[:, h:h + 4, :], down_t16[:, h:h + 4, :]).then_inc(c_down, 1)
                dve.wait_ge(c_x, 16)
                for p in range(STAGES - 1):
                    norms(p)

                def scale(b):
                    for t in range(LT):
                        dve.wait_ge(f_y, b * LT + t + 1)
                        wait(dve, f_o, (b - 1) * LT + t + 1)
                        dve.tensor_tensor(y1[:, t, :], y_ps[t][:, :], ds_n[:, :], ALU.mult).then_inc(f_ys, 1)

                def statistics(b):
                    ts = slice(b * LT, (b + 1) * LT)
                    for t in range(LT):
                        dve.wait_ge(f_ys, b * LT + t + 1)
                        mark(dve.bn_stats(statsF[:, b * LT + t, :], y1[:, t, :]))
                    settle()
                    for t in range(LT):
                        mark(dve.bn_aggr(mvF[:, b * LT + t, :], statsF[:, b * LT + t, :]))
                    settle()
                    rstd_of(mvF[:, ts, 1], mvF[:, ts, 0], rstdF[:, ts], nmrF[:, ts], rtmp, f_r)

                def add(b):
                    for t in range(LT):
                        dve.wait_ge(f_n, b * LT + t + 1)
                        dve.tensor_tensor(xr[:, b * LT + t, :], xr[:, b * LT + t, :], y1[:, t, :], ALU.add).then_inc(f_o, 1)

                def step(b, n, ht, a, k):
                    if b == 0 and k == HT:
                        copy_x2T(LT + 1)
                        copy_x2T(LT + 3)
                    if ht is not None:
                        dve.wait_ge(f_u, n + 1)
                        dve.wait_ge(f_silu, n + 1)
                        wait(dve, f_hl, n - 1)
                        dve.scalar_tensor_tensor(out=hid[:, a, :], in0=u_ps[a][:, :], scalar=us_n[:, bass.ds(ht, 1)],
                                                 in1=silu[:, a, :], op0=ALU.mult, op1=ALU.mult).then_inc(f_h, 1)
                        dve.wait_ge(f_hh, n + 1)
                        dve.tensor_tensor(hidL[:, a, :], hid[:, a, :], hidH[:, a, :].bitcast(F32), ALU.subtract).then_inc(f_hl, 1)
                    if k == HT:
                        scale(b)
                    if b and k == 0:
                        statistics(0)
                    if b == 0 and k == 1:
                        norms(STAGES - 1)
                    if b and k == 1:
                        add(0)

                hidden_steps(dve, step)
                statistics(1)
                add(1)

            @block.gpsimd
            def _(pool):
                pool.tensor_copy(ident16[:, :], identf[:, :]).then_inc(c_ident, 1)
                for t in range(TT):
                    pool.wait_ge(c_hi, t + 1)
                    wait(pool, c_xT, t - 3)
                    pool.tensor_tensor(xh[:, t % 4, 1, :], x2[:, t % 2, :], xh[:, t % 4, 0, :], ALU.subtract).then_inc(c_lo, 1)

            @block.sync
            def _(sp):
                for t in range(TT):
                    sp.wait_ge(f_o, t + 1)
                    sp.dma_start(out[t * P:(t + 1) * P, :], xr[:, t, :]).then_inc(f_st, 16)
                sp.wait_ge(f_st, 16 * TT)


def kernel(L0_attn_x, L0_attn_Wq, L0_attn_bq, L0_attn_Wk, L0_attn_bk, L0_attn_Wv, L0_attn_bv, L0_attn_Wo, L0_attn_bo,
           L0_ffn_gate_w, L0_ffn_gate_scale, L0_ffn_up_w, L0_ffn_up_scale, L0_ffn_down_w, L0_ffn_down_scale):
    import numpy as np
    import concourse.bacc as bacc
    from concourse.bass_utils import run_bass_kernel_spmd

    D = L0_attn_x.shape[-1]

    def turned(w):
        wt = np.asarray(w).T
        return np.ascontiguousarray(wt.reshape(-1, P, wt.shape[1]).transpose(1, 0, 2))

    def columns(v):
        return np.ascontiguousarray(np.asarray(v).reshape(-1, P).T)

    def spread(v):
        return np.ascontiguousarray(np.broadcast_to(np.asarray(v).reshape(1, -1), (P, v.size)))

    arrays = {
        "x": np.ascontiguousarray(np.asarray(L0_attn_x).reshape(-1, D)),
        "wqT": turned(L0_attn_Wq), "wkT": turned(L0_attn_Wk), "wvT": turned(L0_attn_Wv), "woT": turned(L0_attn_Wo),
        "bq": columns(L0_attn_bq), "bk": columns(L0_attn_bk), "bv": spread(L0_attn_bv), "bo": spread(L0_attn_bo),
        "gateT": turned(L0_ffn_gate_w), "upT": turned(L0_ffn_up_w), "downT": turned(L0_ffn_down_w),
        "gate_s": columns(L0_ffn_gate_scale), "up_s": columns(L0_ffn_up_scale), "down_s": spread(L0_ffn_down_scale),
    }
    nc = bacc.Bacc("TRN2", target_bir_lowering=False, num_devices=1)
    args = [nc.dram_tensor(f"in_{n}", a.shape, mybir.dt.from_np(a.dtype), kind="ExternalInput").ap() for n, a in arrays.items()]
    out = nc.dram_tensor("out_0", arrays["x"].shape, F32, kind="ExternalOutput").ap()
    sandwich_block(nc, *args, out)
    r = run_bass_kernel_spmd(nc, [{f"in_{n}": a for n, a in arrays.items()}], core_ids=[0])
    return r.results[0]["out_0"].reshape(np.asarray(L0_attn_x).shape)
```
